# Optimizing a Trainium2 kernel written in Bass

```python
import numpy as np
import jax
import jax.numpy as jnp

def _softmax(x, axis=-1):
    return jax.nn.softmax(x, axis=axis)

def _gelu(x):
    return jax.nn.gelu(x, approximate=True)

def _silu(x):
    return jax.nn.silu(x)

def _sigmoid(x):
    return jax.nn.sigmoid(x)

def _layernorm(x, axis=-1, eps=1e-05):
    m = jnp.mean(x, axis=axis, keepdims=True)
    v = jnp.var(x, axis=axis, keepdims=True)
    return (x - m) / jnp.sqrt(v + eps)

def _scatter_add(tgt, idx, src, axis=0):
    return tgt.at[idx].add(src)

def _segment_sum(src, seg, n):
    return jax.ops.segment_sum(src, seg, n)
kernel_name = 'mk_rec_standalone_d1_rec_r8_b0fd76'

def setup_inputs(seed: int=0):
    np.random.seed(seed)
    _w = jnp.asarray

    def _rec_inputs():
        import jax
        import jax.numpy as jnp
        _rk = jax.random.key(seed)
        r_x = -0.000104943 + 0.999951 * jax.random.normal(jax.random.fold_in(_rk, 1), (512, 64, 768), jnp.float32)
        r_D = jax.random.randint(jax.random.fold_in(_rk, 2), (512,), 0, 4, jnp.int32)
        return (r_x, r_D)
    r_x, r_D = _rec_inputs()

    def _L0_rec_setup():
        import jax, jax.numpy as jnp
        import numpy as np
        B, L, DM, H, E, HD = (512, 64, 768, 4, 8, 384)
        EPS = 1e-05
        key = jax.random.key(seed)
        ks = jax.random.split(key, 10)
        s = lambda k, sh: jax.random.normal(k, sh, jnp.float32) * 0.02
        return dict(x=jax.random.normal(ks[0], (B, L, DM), jnp.float32), D=jax.random.randint(ks[1], (B,), 0, H), aw=s(ks[2], (DM,)), gW1=s(ks[3], (H, DM, HD)), gb1=jnp.zeros((H, HD), jnp.float32), gW2=s(ks[4], (H, HD, E)), gb2=jnp.zeros((H, E), jnp.float32), eW1=s(ks[5], (E, DM, DM)), eb1=jnp.zeros((E, DM), jnp.float32), bn1_g=jnp.ones((E, DM), jnp.float32), bn1_b=jnp.zeros((E, DM), jnp.float32), eW2=s(ks[6], (E, DM, HD)), eb2=jnp.zeros((E, HD), jnp.float32), bn2_g=jnp.ones((E, HD), jnp.float32), bn2_b=jnp.zeros((E, HD), jnp.float32), hW=s(ks[7], (H, HD, 2)), hb=jnp.zeros((H, 2), jnp.float32))
    _L0_rec_all = _L0_rec_setup()
    _L0_rec_in = {k: v for k, v in _L0_rec_all.items() if k in ('aw', 'gW1', 'gb1', 'gW2', 'gb2', 'eW1', 'eb1', 'bn1_g', 'bn1_b', 'eW2', 'eb2', 'bn2_g', 'bn2_b', 'hW', 'hb')}
    del _L0_rec_all
    return {'r_x': r_x, 'r_D': r_D, 'L0_rec_aw': _L0_rec_in['aw'], 'L0_rec_gW1': _L0_rec_in['gW1'], 'L0_rec_gb1': _L0_rec_in['gb1'], 'L0_rec_gW2': _L0_rec_in['gW2'], 'L0_rec_gb2': _L0_rec_in['gb2'], 'L0_rec_eW1': _L0_rec_in['eW1'], 'L0_rec_eb1': _L0_rec_in['eb1'], 'L0_rec_bn1_g': _L0_rec_in['bn1_g'], 'L0_rec_bn1_b': _L0_rec_in['bn1_b'], 'L0_rec_eW2': _L0_rec_in['eW2'], 'L0_rec_eb2': _L0_rec_in['eb2'], 'L0_rec_bn2_g': _L0_rec_in['bn2_g'], 'L0_rec_bn2_b': _L0_rec_in['bn2_b'], 'L0_rec_hW': _L0_rec_in['hW'], 'L0_rec_hb': _L0_rec_in['hb']}

def reference(r_x, r_D, L0_rec_aw, L0_rec_gW1, L0_rec_gb1, L0_rec_gW2, L0_rec_gb2, L0_rec_eW1, L0_rec_eb1, L0_rec_bn1_g, L0_rec_bn1_b, L0_rec_eW2, L0_rec_eb2, L0_rec_bn2_g, L0_rec_bn2_b, L0_rec_hW, L0_rec_hb):
    import jax
    import jax.numpy as jnp

    def _L0_rec_ref(x, D, aw, gW1, gb1, gW2, gb2, eW1, eb1, bn1_g, bn1_b, eW2, eb2, bn2_g, bn2_b, hW, hb):
        import jax, jax.numpy as jnp
        import numpy as np
        B, L, DM, H, E, HD = (512, 64, 768, 4, 8, 384)
        EPS = 1e-05
        mask = x.sum(-1) != 0
        scores = jnp.einsum('bld,d->bl', x, aw)
        scores = jnp.where(mask, scores, -jnp.inf)
        p = jax.nn.softmax(scores, axis=-1)
        feature = jnp.einsum('bl,bld->bd', p, x)
        b = feature.shape[0]
        g_h = jax.nn.relu(jnp.einsum('bd,hdk->bhk', feature, gW1) + gb1)
        g_all = jax.nn.softmax(jnp.einsum('bhk,hke->bhe', g_h, gW2) + gb2, axis=-1)
        gate = g_all[jnp.arange(b), D]
        inv1 = bn1_g / jnp.sqrt(1.0 + EPS)
        h1 = jax.nn.relu((jnp.einsum('bd,edk->ebk', feature, eW1) + eb1[:, None]) * inv1[:, None] + bn1_b[:, None])
        inv2 = bn2_g / jnp.sqrt(1.0 + EPS)
        h2 = jax.nn.relu((jnp.einsum('ebk,eko->ebo', h1, eW2) + eb2[:, None]) * inv2[:, None] + bn2_b[:, None])
        rep = jnp.einsum('be,ebo->bo', gate, h2)
        out_all = jnp.einsum('bo,hoc->bhc', rep, hW) + hb
        out = out_all[jnp.arange(b), D]
        return jax.nn.softmax(out, axis=-1)
    y = _L0_rec_ref(r_x, r_D, L0_rec_aw, L0_rec_gW1, L0_rec_gb1, L0_rec_gW2, L0_rec_gb2, L0_rec_eW1, L0_rec_eb1, L0_rec_bn1_g, L0_rec_bn1_b, L0_rec_eW2, L0_rec_eb2, L0_rec_bn2_g, L0_rec_bn2_b, L0_rec_hW, L0_rec_hb)
    return y

_drawn_inputs = setup_inputs


def setup_inputs(seed=0):
    import zlib

    import numpy as np

    out = dict(_drawn_inputs(seed))
    spreads = {'L0_rec_gb1': (0.0, 0.8),
     'L0_rec_gb2': (0.0, 2.0),
     'L0_rec_eb1': (0.0, 0.8),
     'L0_rec_bn1_g': (1.0, 0.6),
     'L0_rec_bn1_b': (0.0, 0.8),
     'L0_rec_eb2': (0.0, 2.0),
     'L0_rec_bn2_g': (1.0, 0.6),
     'L0_rec_bn2_b': (0.0, 2.0),
     'L0_rec_hb': (0.0, 2.0)}
    factors = {'r_x': 8.0,
     'L0_rec_aw': 8.0,
     'L0_rec_gW1': 8.0,
     'L0_rec_gW2': 8.0,
     'L0_rec_eW1': 8.0,
     'L0_rec_eW2': 8.0,
     'L0_rec_hW': 2.767}
    for name, (base, spread) in spreads.items():
        noise = np.random.default_rng([zlib.crc32(name.encode()), seed]).standard_normal(out[name].shape)
        drawn = base * np.exp(spread * noise) if base else spread * noise
        out[name] = jnp.asarray(drawn.astype(out[name].dtype))
    for name, factor in factors.items():
        out[name] = (out[name] * factor).astype(out[name].dtype)
    return out
```

```python
from contextlib import ExitStack

import concourse.bass as bass
from concourse import mybir

F32 = mybir.dt.float32
F32R = mybir.dt.float32r
BF16 = mybir.dt.bfloat16
I32 = mybir.dt.int32
ALU = mybir.AluOpType
ACT = mybir.ActivationFunctionType
AX = mybir.AxisListType

P = 128
EPS = 1e-05
BN_SCALE = float((1.0 + EPS) ** -0.5)

CHUNK = 256
CG = 4
ROUND_TILES = 8
RING_ROUNDS = 4
BLOCK_ROUNDS = 8
RAW = 4
SPLIT = 3
AHEAD = 2
KU = 3
MT = 3
UNIT_COLS = MT * P
WIN = 30
ZB = 4
BODY = 4
EU = 6


def rec_kernel(nc, x, D, aw, gW1, gb1, gW2, gb2, eW1, eb1, bn1_g, bn1_b, eW2, eb2, bn2_g, bn2_b, hW, hb, out):
    B, L, DM = x.shape
    H, _, HD = gW1.shape
    E = eW1.shape[0]
    KT = DM // P
    HT = HD // P
    NCH = B // CHUNK
    CB = CHUNK // P
    NBLK = B // P
    GU = 2 * H
    UNITS = GU + EU * E
    BU = BODY * EU
    ITERS = E // BODY
    assert 2 * L == P and KT == 2 * KU and HD == UNIT_COLS and ITERS == CB
    assert MT * (UNITS // 2) % ZB == 0 and MT * (BU // 2) % ZB == 0
    assert UNITS % RAW == 0 and GU % RAW == 0 and BU % RAW == 0 and BU % SPLIT == 0

    x_v = x.rearrange("(b j r i h) l d -> b r (h l) j i d", j=CG, r=BLOCK_ROUNDS, i=2, h=2)
    gW1_v = gW1.rearrange("h (p k) n -> h p k n", k=KT)
    eW1_v = eW1.rearrange("e (p k) n -> e p k n", k=KT)
    eW2_v = eW2.rearrange("e (k p) n -> e p k n", p=P)

    with ExitStack() as ctx:
        def sb(name, shape, dt=F32):
            return ctx.enter_context(nc.sbuf_tensor(name, shape, dt))

        def psum(name, shape):
            return ctx.enter_context(nc.psum_tensor(name, shape, F32))

        def sem(name):
            return ctx.enter_context(nc.semaphore(name))

        xring = sb("xring", [P, RING_ROUNDS, CG, 2, DM])
        aw_bc = sb("aw_bc", [P, DM])
        prod_out = sb("prod_out", [P, 2, DM], BF16)
        copy_out = sb("copy_out", [P, 2, DM], BF16)
        score = sb("score", [P, 2, ROUND_TILES])
        rowsum = sb("rowsum", [P, 2, ROUND_TILES])
        penalty = sb("penalty", [P, ROUND_TILES])
        masked = sb("masked", [P, 2, ROUND_TILES])
        neg_max = sb("neg_max", [ROUND_TILES, 2, 2])
        expsum = sb("expsum", [ROUND_TILES, 2])
        recip = sb("recip", [ROUND_TILES, 2])
        prob = sb("prob", [P, 2, L])
        pwin = sb("pwin", [P, ROUND_TILES, WIN + 32])
        rows = sb("rows", [P, DM])
        feat_hi = sb("feat_hi", [P, NCH, KT, CHUNK], F32R)
        feat_lo = sb("feat_lo", [P, NCH, KT, CHUNK], F32R)
        ident = sb("ident", [P, P])
        wraw = sb("wraw", [P, RAW, KU, UNIT_COLS])
        whi = sb("whi", [P, SPLIT, KU, UNIT_COLS], F32R)
        wlo = sb("wlo", [P, SPLIT, KU, UNIT_COLS], F32R)
        h1 = sb("h1", [P, KT, CHUNK])
        h1_hi = sb("h1_hi", [P, KT, CHUNK], F32R)
        h1_lo = sb("h1_lo", [P, KT, CHUNK], F32R)
        h2 = sb("h2", [P, HT, CHUNK])
        rep = sb("rep", [P, HT, CHUNK])
        gW2_sb = sb("gW2_sb", [P, H * HT, E])
        hW_sb = sb("hW_sb", [P, HT, H, 2])
        gb2_bc = sb("gb2_bc", [P, H, E])
        hb_bc = sb("hb_bc", [P, H, 2])
        D_i = sb("D_i", [P, NBLK], I32)
        D_f = sb("D_f", [P, NBLK])
        head_is = sb("head_is", [P, NBLK, H])
        ones = sb("ones", [E, P])
        gl = sb("gl", [P, CB, E])
        gmax = sb("gmax", [P, CB])
        gexp = sb("gexp", [P, CB, E])
        gsum = sb("gsum", [P, CB])
        grec = sb("grec", [P, CB])
        gate = sb("gate", [P, CB, E])
        gateT = sb("gateT", [E, CHUNK])
        osel = sb("osel", [P, 2, H, 2])
        ol = sb("ol", [P, CB, 2])
        omax = sb("omax", [P, CB])
        oexp = sb("oexp", [P, CB, 2])
        osum = sb("osum", [P, CB])
        orec = sb("orec", [P, CB])
        out_sb = sb("out_sb", [P, NBLK, 2])
        scale = sb("scale", [P, E * (KT + HT)])
        bias = sb("bias", [P, E * (KT + HT) + H * HT])
        prm = rows[:, 0:2 * P].rearrange("p (a n) -> p a n", a=2)
        gate_e = rows[0:E, DM - CHUNK:DM]
        prm_rows = h2[:, 0, 0:2 * P].rearrange("p (a n) -> p a n", a=2)
        glogit = h2[:, 1, :]
        gsel = h2[:, 2, 0:CB * H * E].rearrange("p (b h e) -> p b h e", b=CB, h=H)

        feat_ps = psum("feat_ps", [P, 2, 512])
        z_ps = psum("z_ps", [P, ZB, 512])
        soft_ps = psum("soft_ps", [P, 512])
        exps = soft_ps[0:ROUND_TILES, 2 * P:3 * P].rearrange("t (h l) -> t h l", h=2)
        turn_ps = psum("turn_ps", [P, 512])
        logit_ps = turn_ps[:, CHUNK:2 * CHUNK]
        gate_bc = turn_ps[:, 0:CHUNK]

        aw_loaded = sem("aw_loaded")
        setup_loaded = sem("setup_loaded")
        x_loaded = [[sem(f"x_loaded{r}_{j}") for j in range(2)] for r in range(RING_ROUNDS)]
        w_loaded = [sem(f"w_loaded{s}") for s in range(RAW)]
        ident_zero = sem("ident_zero")
        ident_ready = sem("ident_ready")
        zeroed = sem("zeroed")
        link_dve = sem("link_dve")
        params_ready = sem("params_ready")
        scored = sem("scored")
        summed = sem("summed")
        pen_ready = sem("pen_ready")
        mask_ready = sem("mask_ready")
        scores_turned = sem("scores_turned")
        max_ready = sem("max_ready")
        exp_ready = sem("exp_ready")
        recip_ready = sem("recip_ready")
        prob_ready = sem("prob_ready")
        prob_turned = sem("prob_turned")
        pwin_ready = sem("pwin_ready")
        feat_added = sem("feat_added")
        rows_a = sem("rows_a")
        rows_b = sem("rows_b")
        turned = sem("turned")
        turned_hi = sem("turned_hi")
        turned_read = sem("turned_read")
        hi_ready = sem("hi_ready")
        lo_ready = sem("lo_ready")
        half_used = sem("half_used")
        z_ready = sem("z_ready")
        z_read = sem("z_read")
        h1_hi_ready = sem("h1_hi_ready")
        h1_ready = sem("h1_ready")
        logits_ready = sem("logits_ready")
        gl_ready = sem("gl_ready")
        gmax_ready = sem("gmax_ready")
        gexp_ready = sem("gexp_ready")
        gate_ready = sem("gate_ready")
        gateT_ready = sem("gateT_ready")
        gate_e_ready = sem("gate_e_ready")
        gate_bc_ready = sem("gate_bc_ready")
        gated_ready = sem("gated_ready")
        rep_zeroed = sem("rep_zeroed")
        rep_added = sem("rep_added")
        out_logits = sem("out_logits")
        omax_ready = sem("omax_ready")
        oexp_ready = sem("oexp_ready")
        out_ready = sem("out_ready")
        stored = sem("stored")


        def tiles(it, panel, m):
            return it * (MT * BU // 2) + (MT * panel + m + 1)

        def wait_unit_used(eng, it, u0):
            if u0 % 2 == 0:
                eng.wait_ge(half_used, it * (BU // 2) + (u0 // 2 + 1))
            else:
                eng.wait_ge(z_ready, tiles(it, u0 // 2, MT - 1))

        def is_split(u0):
            c, n = divmod(u0, UNITS)
            return c > 0 or n < GU or (n - GU) % EU < EU - 2

        def splits(it, u0):
            c, n = divmod(u0, UNITS)
            if c == 0 and n >= GU:
                q, k = divmod(n - GU, EU)
                return it * ((EU - 2) * BODY) + (GU + (EU - 2) * q + k + 1)
            return it * BU + (u0 + 1 - min(c, 1) * 2 * E)

        N1, N2 = E * KT, E * HT
        GATE0 = [UNITS * c for c in range(NCH)]
        EXP0 = [UNITS * c + GU for c in range(NCH)]
        FEAT_TURN = [(2 * CB + 2) * c + (c > 0) for c in range(NCH)]
        PRM_TURN = 2 * CB
        GATE_TURN = [FEAT_TURN[c] + 2 * CB + (c == 0) for c in range(NCH)]
        FEAT_READ = [2 * CB * c + (c > 0) for c in range(NCH)]

        def x_slots(s):
            r, third = divmod(s, 3)
            return r, third, range(3 * third, min(3 * third + 3, ROUND_TILES))

        block = ctx.enter_context(nc.Block())

        @block.sync
        def _(sp):
            def load_round(b, r, wait):
                if wait:
                    sp.wait_ge(feat_added, b * BLOCK_ROUNDS + (r + 1 - RING_ROUNDS))
                for j in range(CG):
                    sp.dma_start(xring[:, r % RING_ROUNDS, j, :, :],
                                 x_v[b, r, :, j, :, :]).then_inc(x_loaded[r % RING_ROUNDS][j // 2], 16)

            for r in range(RING_ROUNDS):
                load_round(0, r, False)
            sp.wait_ge(zeroed, 1)
            for a, at, src in ((0, 0, eb1), (0, N1, bn1_g), (0, 2 * N1, eb2), (1, 0, bn1_b), (1, N1, bn2_g),
                               (1, N1 + N2, bn2_b), (1, N1 + 2 * N2, gb1)):
                src = src.rearrange("e (m p) -> (e m) p", p=P)
                sp.dma_start(prm_rows[at:at + src.shape[0], a, :], src).then_inc(setup_loaded, 16)
            sp.dma_start(D_i[:, :], D.rearrange("(b p) -> p b", p=P),
                         allow_slow_non_contiguous=True).then_inc(setup_loaded, 16)
            sp.dma_start(gb2_bc[:, :, :], gb2.partition_broadcast(P)).then_inc(setup_loaded, 16)
            sp.dma_start(hb_bc[:, :, :], hb.partition_broadcast(P)).then_inc(setup_loaded, 16)
            sp.dma_start(gW2_sb[:, :, :], gW2.rearrange("h (m p) e -> p (h m) e", p=P)).then_inc(setup_loaded, 16)
            for m in range(HT):
                sp.dma_start(hW_sb[:, m, :, :],
                             hW[:, m * P:(m + 1) * P, :].rearrange("h p c -> p h c")).then_inc(setup_loaded, 16)
            for r in range(RING_ROUNDS, BLOCK_ROUNDS):
                load_round(0, r, True)
            with sp.Fori(1, NBLK) as b:
                for r in range(BLOCK_ROUNDS):
                    load_round(b, r, True)
            sp.wait_ge(out_ready, NCH)
            sp.dma_start(out.rearrange("(b p) c -> p b c", p=P), out_sb[:, :, :]).then_inc(stored, 16)
            sp.wait_ge(stored, 16)

        @block.gpsimd
        def _(pool):
            nc.gpsimd.memset(ident[:, :], 0.0).then_inc(ident_zero, 1)
            pool.wait_ge(ident_zero, 1)
            nc.gpsimd.affine_select(out=ident[:, :], in_=ident[:, :], compare_op=ALU.not_equal, fill=1.0,
                                    base=0, pattern=[[-1, P]], channel_multiplier=1).then_inc(ident_ready, 1)

            def load_unit(it, u0, src):
                if u0 >= RAW:
                    wait_raw_used(it, u0 - RAW)
                pool.dma_start(wraw[:, u0 % RAW, :, :], src).then_inc(w_loaded[u0 % RAW], 16)

            def wait_raw_used(it, u0):
                if is_split(u0) and not (u0 < GU and not isinstance(it, int)):
                    pool.wait_ge(lo_ready, splits(it, u0))
                else:
                    wait_unit_used(pool, it, u0)

            def gate_unit(u0, n):
                head, half = divmod(n, 2)
                load_unit(0, u0, gW1_v[head, :, KU * half:KU * half + KU, :])

            for c in range(NCH):
                for n in range(GU):
                    gate_unit(GATE0[c] + n, n)
                with pool.Fori(0, ITERS) as it:
                    for n in range(BU):
                        q, k = divmod(n, EU)
                        panel, half = divmod(k, 2)
                        ks = slice(KU * half, KU * half + KU)
                        if panel < 2:
                            src = eW1_v[it * BODY + q, :, ks, UNIT_COLS * panel:UNIT_COLS * (panel + 1)]
                        else:
                            src = eW2_v[it * BODY + q, :, ks, :]
                        load_unit(it, EXP0[c] + n, src)
            for n in range(AHEAD):
                gate_unit(NCH * UNITS + n, n)
            for n in range(AHEAD):
                u0 = NCH * UNITS + n
                pool.wait_ge(w_loaded[u0 % RAW], 16 * (u0 // RAW + 1))

        @block.scalar
        def _(act):
            act.dma_start(aw_bc[:, :], aw.partition_broadcast(P)).then_inc(aw_loaded, 16)

            def split_hi(it, u0):
                if not is_split(u0):
                    return
                act.wait_ge(w_loaded[u0 % RAW], it * (16 * BU // RAW) + 16 * (u0 // RAW + 1))
                if u0 >= SPLIT:
                    wait_unit_used(act, it, u0 - SPLIT)
                nc.scalar.activation(whi[:, u0 % SPLIT, :, :], wraw[:, u0 % RAW, :, :], ACT.Copy).then_inc(hi_ready, 1)

            def sum_rows(b, r, ts):
                for t in ts:
                    j, i = divmod(t, 2)
                    if t == 0 or t == 4:
                        act.wait_ge(x_loaded[r % RING_ROUNDS][j // 2], b * 64 + 32 * (r // RING_ROUNDS + 1))
                    at = r * ROUND_TILES + t
                    if at >= 2:
                        act.wait_ge(summed, b * (BLOCK_ROUNDS * ROUND_TILES) + (at - 1))
                    if t == 0 and r >= 2:
                        act.wait_ge(mask_ready, b * BLOCK_ROUNDS + (r - 1))
                    nc.scalar.activation(copy_out[:, t % 2, :], xring[:, r % RING_ROUNDS, j, i, :], ACT.Copy,
                                         accum_out=rowsum[:, r % 2, t:t + 1]).then_inc(summed, 1)

            def softmax_exp(b, r):
                act.wait_ge(max_ready, b * BLOCK_ROUNDS + (r + 1))
                for h in range(2):
                    last = nc.scalar.activation(exps[:, h, :], soft_ps[0:ROUND_TILES, L * h:L * h + L], ACT.Exp,
                                                bias=neg_max[:, r % 2, h:h + 1], accum_out=expsum[:, h:h + 1])
                last.then_inc(exp_ready, 1)

            def block_end(b, it, c, blk):
                act.wait_ge(feat_added, b * BLOCK_ROUNDS + BLOCK_ROUNDS)
                nc.scalar.activation(rows[:, 0:DM // 2], feat_ps[:, 0, 0:DM // 2], ACT.Copy).then_inc(rows_a, 1)
                for g in range(2):
                    act.wait_ge(turned, it * 2 + (FEAT_TURN[c] + g + 1))
                    nc.scalar.activation(feat_hi[:, c, KU * g:KU * g + KU, blk],
                                         turn_ps[:, 0:KU * P].rearrange("p (k n) -> p k n", k=KU),
                                         ACT.Copy).then_inc(turned_hi, 1)

            def read_h1(it, q, panel0, c, ms):
                panel = EXP0[c] // 2 + 3 * q + panel0
                for m in ms:
                    t = MT * panel0 + m
                    act.wait_ge(z_ready, tiles(it, panel, m))
                    if c and q:
                        act.wait_ge(h1_ready, it * (KT * BODY) + (KT * (q - 1) + t + 1))
                    col = bass.ds(it * (KT * BODY) + (KT * q + t), 1)
                    nc.scalar.activation(h1[:, t, :], z_ps[:, (MT * panel + m) % ZB, 0:CHUNK], ACT.Relu,
                                         bias=bias[:, col], scale=scale[:, col]).then_inc(z_read, 1)

            def read_h2(it, q, c, ms):
                panel = EXP0[c] // 2 + 3 * q + 2
                if ms[0] == 0:
                    if c or q:
                        act.wait_ge(rep_added, it * BODY + (E * c + q))
                    else:
                        act.wait_ge(logits_ready, H)
                for m in ms:
                    act.wait_ge(z_ready, tiles(it, panel, m))
                    col = bass.ds(it * (HT * BODY) + (E * KT + HT * q + m), 1)
                    nc.scalar.activation(h2[:, m, :], z_ps[:, (MT * panel + m) % ZB, 0:CHUNK], ACT.Relu,
                                         bias=bias[:, col], scale=scale[:, col]).then_inc(z_read, 1)

            def read_gate(c, head):
                panel = GATE0[c] // 2 + head
                if head:
                    act.wait_ge(logits_ready, H * c + head)
                elif c:
                    act.wait_ge(rep_added, E * c)
                for m in range(MT):
                    act.wait_ge(z_ready, tiles(0, panel, m))
                    at = N1 + N2 + HT * head + m
                    nc.scalar.activation(h2[:, m, :], z_ps[:, (MT * panel + m) % ZB, 0:CHUNK], ACT.Relu,
                                         bias=bias[:, at:at + 1]).then_inc(z_read, 1)

            def slots(c, it, xb, experts):
                for s in range(BU):
                    q, k = divmod(s, EU)
                    if experts:
                        split_hi(it, EXP0[c] + s + AHEAD)
                        if k in (2, 4):
                            read_h1(it, q, k // 2 - 1, c, (2,))
                        if k == 0 and q:
                            read_h2(it, q - 1, c, (2,))
                    if xb is not None:
                        r, third, ts = x_slots(s)
                        sum_rows(xb, r, ts)
                        if third == 1 and r:
                            softmax_exp(xb, r - 1)
                    if experts and k in (1, 3):
                        read_h1(it, q, k // 2, c, (0, 1))
                    if experts and k == 5:
                        read_h2(it, q, c, (0, 1))
                if experts:
                    read_h2(it, BODY - 1, c, (2,))
                if xb is not None:
                    softmax_exp(xb, BLOCK_ROUNDS - 1)

            def gate_stage(c):
                act.wait_ge(params_ready, 1)
                for n in range(GU):
                    split_hi(0, GATE0[c] + n + AHEAD)
                    if c and n == 3:
                        head_exp(c - 1)
                    if n % 2:
                        read_gate(c, n // 2)
                act.wait_ge(gmax_ready, c + 1)
                for b in range(CB):
                    last = nc.scalar.activation(gexp[:, b, :], gl[:, b, :], ACT.Exp, bias=gmax[:, b:b + 1],
                                                accum_out=gsum[:, b:b + 1])
                last.then_inc(gexp_ready, 1)

            def head_exp(c):
                act.wait_ge(omax_ready, c + 1)
                for b in range(CB):
                    last = nc.scalar.activation(oexp[:, b, :], ol[:, b, :], ACT.Exp, bias=omax[:, b:b + 1],
                                                accum_out=osum[:, b:b + 1])
                last.then_inc(oexp_ready, 1)

            def blk(it):
                return bass.ds(it * P, P)

            for n in range(AHEAD):
                split_hi(0, n)
            with act.Fori(0, CB) as it:
                slots(0, it, it, False)
                block_end(it, it, 0, blk(it))
            gate_stage(0)
            with act.Fori(0, ITERS) as it:
                slots(0, it, it + CB, True)
                block_end(it + CB, it, 1, blk(it))
            gate_stage(1)
            with act.Fori(0, ITERS) as it:
                slots(1, it, None, True)
            head_exp(1)

        @block.vector
        def _(dve):
            links = [0]

            def link(ins):
                links[0] += 1
                ins.then_inc(link_dve, 1)
                dve.wait_ge(link_dve, links[0])

            nc.vector.memset(h2[:, :, :], 0.0).then_inc(zeroed, 1)
            nc.vector.memset(pwin[:, :, :], 0.0)
            nc.vector.memset(ones[:, :], 1.0)
            nc.vector.memset(prob[:, :, :], 0.0)
            nc.vector.memset(rep[:, :, :], 0.0).then_inc(rep_zeroed, 1)

            def split_lo(it, u0):
                if not is_split(u0):
                    return
                dve.wait_ge(hi_ready, splits(it, u0))
                nc.vector.tensor_tensor(wlo[:, u0 % SPLIT, :, :], wraw[:, u0 % RAW, :, :],
                                        whi[:, u0 % SPLIT, :, :].bitcast(F32), ALU.subtract).then_inc(lo_ready, 1)

            def score_tile(b, r, t):
                j, i = divmod(t, 2)
                if t == 0 or t == 4:
                    dve.wait_ge(x_loaded[r % RING_ROUNDS][j // 2], b * 64 + 32 * (r // RING_ROUNDS + 1))
                at = r * ROUND_TILES + t
                if at >= 2:
                    dve.wait_ge(scored, b * (BLOCK_ROUNDS * ROUND_TILES) + (at - 1))
                nc.vector.tensor_tensor_reduce(
                    out=prod_out[:, t % 2, :], in0=xring[:, r % RING_ROUNDS, j, i, :], in1=aw_bc[:, :], scale=1.0,
                    scalar=0.0, op0=ALU.mult, op1=ALU.add, accum_out=score[:, r % 2, t:t + 1]).then_inc(scored, 1)

            def mask_scores(b, r):
                n = b * BLOCK_ROUNDS + (r + 1)
                dve.wait_ge(summed, n * ROUND_TILES)
                nc.vector.tensor_scalar(penalty[:, :], rowsum[:, r % 2, :], 0.0, -3e38, ALU.is_equal,
                                        ALU.mult).then_inc(pen_ready, 1)
                dve.wait_ge(pen_ready, n)
                dve.wait_ge(scored, n * ROUND_TILES)
                nc.vector.scalar_tensor_tensor(out=masked[:, r % 2, :], in0=penalty[:, :], scalar=3.0,
                                               in1=score[:, r % 2, :], op0=ALU.mult,
                                               op1=ALU.add).then_inc(mask_ready, 1)

            def softmax_max(b, r):
                dve.wait_ge(scores_turned, b * BLOCK_ROUNDS + (r + 1))
                nc.vector.tensor_reduce(neg_max[:, r % 2, :],
                                        soft_ps[0:ROUND_TILES, 0:P].rearrange("t (h l) -> t h l", h=2),
                                        AX.X, ALU.max, negate=True).then_inc(max_ready, 1)

            def softmax_norm(b, r):
                n = b * BLOCK_ROUNDS + (r + 1)
                dve.wait_ge(exp_ready, n)
                nc.vector.reciprocal(recip[:, :], expsum[:, :]).then_inc(recip_ready, 1)
                dve.wait_ge(recip_ready, n)
                nc.vector.tensor_tensor(prob[0:ROUND_TILES, :, :], exps[:, :, :],
                                        recip[:, :].unsqueeze(2).to_broadcast([ROUND_TILES, 2, L]),
                                        ALU.mult).then_inc(prob_ready, 1)

            def place_probs(b, r):
                n = b * BLOCK_ROUNDS + r
                dve.wait_ge(prob_turned, n + 1)
                if r:
                    dve.wait_ge(feat_added, n)
                for h in range(2):
                    p = slice(L * h, L * h + L)
                    last = nc.vector.tensor_copy(pwin[p, :, WIN + h],
                                                 soft_ps[p, P:P + ROUND_TILES])
                last.then_inc(pwin_ready, 1)

            def block_end(b, it, c, blk):
                dve.wait_ge(feat_added, b * BLOCK_ROUNDS + BLOCK_ROUNDS)
                nc.vector.tensor_copy(rows[:, DM // 2:DM], feat_ps[:, 1, 0:DM // 2]).then_inc(rows_b, 1)
                for g in range(2):
                    dve.wait_ge(turned_hi, it * 2 + (2 * CB * c + g + 1))
                    ks = slice(KU * g, KU * g + KU)
                    nc.vector.tensor_tensor(feat_lo[:, c, ks, blk],
                                            turn_ps[:, 0:KU * P].rearrange("p (k n) -> p k n", k=KU),
                                            feat_hi[:, c, ks, blk].bitcast(F32),
                                            ALU.subtract).then_inc(turned_read, 1)

            def split_h1(it, q, panel0, c, m):
                panel = EXP0[c] // 2 + 3 * q + panel0
                t = MT * panel0 + m
                dve.wait_ge(z_read, tiles(it, panel, m))
                nc.vector.tensor_copy(h1_hi[:, t, :], h1[:, t, :]).then_inc(h1_hi_ready, 1)
                dve.wait_ge(h1_hi_ready, it * (KT * BODY) + (KT * q + t + 1))
                nc.vector.tensor_tensor(h1_lo[:, t, :], h1[:, t, :], h1_hi[:, t, :].bitcast(F32),
                                        ALU.subtract).then_inc(h1_ready, 1)

            def pick_gate(it, q, c):
                n = E * c + q
                if n:
                    dve.wait_ge(gate_bc_ready, it * BODY + n)
                nc.vector.tensor_scalar(gate_e, gateT[:, :], ident[0:E, bass.ds(it * BODY + q, 1)],
                                        None, ALU.mult).then_inc(gate_e_ready, 1)

            def add_expert(it, q, c):
                n = E * c + q
                panel = EXP0[c] // 2 + 3 * q + 2
                dve.wait_ge(gate_bc_ready, it * BODY + (n + 1))
                if n:
                    dve.wait_ge(rep_added, it * BODY + n)
                dve.wait_ge(z_read, tiles(it, panel, MT - 1))
                nc.vector.tensor_tensor(h2[:, :, :], h2[:, :, :],
                                        gate_bc.unsqueeze(1).to_broadcast([P, HT, CHUNK]),
                                        ALU.mult).then_inc(gated_ready, 1)
                dve.wait_ge(gated_ready, it * BODY + (n + 1))
                nc.vector.tensor_tensor(rep[:, :, :], rep[:, :, :], h2[:, :, :], ALU.add).then_inc(rep_added, 1)

            def x_third(b, r, third, scoring):
                tiles_of = x_slots(3 * r + third)[2] if scoring else ()
                steps = {0: [(place_probs, r - 2), (mask_scores, r - 1)],
                         1: [(softmax_max, r - 1)],
                         2: [(softmax_norm, r - 1)]}[third]
                for n, t in enumerate(tiles_of):
                    score_tile(b, r, t)
                    yield
                    if n == 0:
                        for step, of in steps:
                            if of >= 0:
                                step(b, of)
                if not tiles_of:
                    for step, of in steps:
                        step(b, of)

            def slots(c, it, xb, experts):
                for s in range(BU):
                    q, k = divmod(s, EU)
                    h1_tiles = [0, 1, 2] if experts and c and k in (2, 4) else []
                    if experts:
                        split_lo(it, EXP0[c] + s + AHEAD)
                    if xb is not None:
                        r, third, _ = x_slots(s)
                        for _ in x_third(xb, r, third, True):
                            if h1_tiles:
                                split_h1(it, q, k // 2 - 1, c, h1_tiles.pop(0))
                    for m in h1_tiles:
                        split_h1(it, q, k // 2 - 1, c, m)
                    if experts and k == 2:
                        pick_gate(it, q, c)
                    if experts and k == 0 and q:
                        add_expert(it, q - 1, c)
                if xb is not None:
                    for third in range(3):
                        for _ in x_third(xb, BLOCK_ROUNDS, third, False):
                            pass
                if experts:
                    add_expert(it, BODY - 1, c)
                if xb is not None:
                    place_probs(xb, BLOCK_ROUNDS - 1)

            def head_softmax(c):
                dve.wait_ge(out_logits, c + 1)
                for b in range(CB):
                    link(nc.vector.tensor_tensor(osel[:, b, :, :],
                                                 logit_ps[:, 8 * b:8 * b + 2 * H].rearrange("p (h c) -> p h c", c=2),
                                                 hb_bc[:, :, :], ALU.add))
                    link(nc.vector.tensor_tensor(osel[:, b, :, :], osel[:, b, :, :],
                                                 head_is[:, CB * c + b, :].unsqueeze(2).to_broadcast([P, H, 2]),
                                                 ALU.mult))
                    link(nc.vector.tensor_reduce(ol[:, b, :], osel[:, b, :, :].rearrange("p h c -> p c h"),
                                                 AX.X, ALU.add))
                nc.vector.tensor_reduce(omax[:, :], ol[:, :, :], AX.X, ALU.max, negate=True).then_inc(omax_ready, 1)
                dve.wait_ge(oexp_ready, c + 1)
                link(nc.vector.reciprocal(orec[:, :], osum[:, :]))
                nc.vector.tensor_tensor(out_sb[:, CB * c:CB * c + CB, :], oexp[:, :, :],
                                        orec[:, :].unsqueeze(2).to_broadcast([P, CB, 2]),
                                        ALU.mult).then_inc(out_ready, 1)

            def gate_stage(c):
                for n in range(GU):
                    split_lo(0, GATE0[c] + n + AHEAD)
                    if c and n == 3:
                        head_softmax(c - 1)
                        nc.vector.memset(rep[:, :, :], 0.0).then_inc(rep_zeroed, 1)
                dve.wait_ge(logits_ready, H * (c + 1))
                for h in range(H):
                    rows_h = slice(32 * h, 32 * h + E)
                    last = nc.vector.tensor_copy(glogit[rows_h, :], logit_ps[rows_h, :])
                last.then_inc(gl_ready, 1)
                dve.wait_ge(turned, GATE_TURN[c] + 1)
                for b in range(CB):
                    turned_b = turn_ps[:, P * b:P * b + P].rearrange("p (h e) -> p h e", h=H)
                    link(nc.vector.tensor_tensor(gsel[:, b, :, :], turned_b[:, :, 0:E], gb2_bc[:, :, :], ALU.add))
                    link(nc.vector.tensor_tensor(gsel[:, b, :, :], gsel[:, b, :, :],
                                                 head_is[:, CB * c + b, :].unsqueeze(2).to_broadcast([P, H, E]),
                                                 ALU.mult))
                    link(nc.vector.tensor_reduce(gl[:, b, :], gsel[:, b, :, :].rearrange("p h e -> p e h"),
                                                 AX.X, ALU.add))
                nc.vector.tensor_reduce(gmax[:, :], gl[:, :, :], AX.X, ALU.max, negate=True).then_inc(gmax_ready, 1)
                dve.wait_ge(gexp_ready, c + 1)
                link(nc.vector.reciprocal(grec[:, :], gsum[:, :]))
                nc.vector.tensor_tensor(gate[:, :, :], gexp[:, :, :],
                                        grec[:, :].unsqueeze(2).to_broadcast([P, CB, E]),
                                        ALU.mult).then_inc(gate_ready, 1)
                dve.wait_ge(turned, GATE_TURN[c] + 2)
                nc.vector.tensor_copy(gateT[:, :], turn_ps[0:E, 0:CHUNK]).then_inc(gateT_ready, 1)
                dve.wait_ge(gateT_ready, c + 1)
                if c:
                    dve.wait_ge(rep_zeroed, 2)

            def blk(it):
                return bass.ds(it * P, P)

            for n in range(AHEAD):
                split_lo(0, n)
            dve.wait_ge(aw_loaded, 16)
            with dve.Fori(0, CB) as it:
                slots(0, it, it, False)
                block_end(it, it, 0, blk(it))
            dve.wait_ge(setup_loaded, 16 * 14)
            link(nc.vector.tensor_copy(D_f[:, :], D_i[:, :]))
            for h in range(H):
                nc.vector.tensor_scalar(head_is[:, :, h], D_f[:, :], float(h), None, ALU.is_equal)
            dve.wait_ge(turned, PRM_TURN + 1)
            nc.vector.tensor_copy(prm[:, 0, 0:2 * N1 + N2], turn_ps[:, 0:2 * N1 + N2])
            nc.vector.tensor_copy(prm[:, 1, 0:N1 + 2 * N2 + H * HT],
                                  turn_ps[:, P:P + N1 + 2 * N2 + H * HT]).then_inc(turned_read, 1)
            dve.wait_ge(turned_read, PRM_TURN + 1)
            nc.vector.tensor_scalar(scale[:, 0:N1], prm[:, 0, N1:2 * N1], BN_SCALE, None, ALU.mult)
            link(nc.vector.tensor_scalar(scale[:, N1:N1 + N2], prm[:, 1, N1:N1 + N2], BN_SCALE, None, ALU.mult))
            nc.vector.tensor_tensor(bias[:, 0:N1], prm[:, 0, 0:N1], scale[:, 0:N1], ALU.mult)
            link(nc.vector.tensor_tensor(bias[:, N1:N1 + N2], prm[:, 0, 2 * N1:2 * N1 + N2], scale[:, N1:N1 + N2],
                                         ALU.mult))
            nc.vector.tensor_tensor(bias[:, 0:N1], bias[:, 0:N1], prm[:, 1, 0:N1], ALU.add)
            nc.vector.tensor_tensor(bias[:, N1:N1 + N2], bias[:, N1:N1 + N2],
                                    prm[:, 1, N1 + N2:N1 + 2 * N2], ALU.add)
            nc.vector.tensor_copy(bias[:, N1 + N2:N1 + N2 + H * HT],
                                  prm[:, 1, N1 + 2 * N2:N1 + 2 * N2 + H * HT]).then_inc(params_ready, 1)
            gate_stage(0)
            with dve.Fori(0, ITERS) as it:
                slots(0, it, it + CB, True)
                block_end(it + CB, it, 1, blk(it))
            gate_stage(1)
            with dve.Fori(0, ITERS) as it:
                slots(1, it, None, True)
            head_softmax(1)

        @block.tensor
        def _(pe):
            def products(psum_tile, w_hi, w_lo, a_hi, a_lo, first, last):
                nc.tensor.matmul(psum_tile, w_hi, a_hi, start=first, stop=False)
                nc.tensor.matmul(psum_tile, w_hi, a_lo, start=False, stop=False)
                return nc.tensor.matmul(psum_tile, w_lo, a_hi, start=False, stop=last)

            def unit(it, u0, a_hi, a_lo, h1_at=None):
                panel, half = divmod(u0, 2)
                slot = u0 % SPLIT
                if is_split(u0):
                    pe.wait_ge(lo_ready, splits(it, u0))
                else:
                    pe.wait_ge(w_loaded[u0 % RAW], it * (16 * BU // RAW) + 16 * (u0 // RAW + 1))
                for m in range(MT):
                    z = z_ps[:, (MT * panel + m) % ZB, 0:CHUNK]
                    cols = slice(P * m, P * m + P)
                    if half == 0 and MT * panel + m >= ZB:
                        pe.wait_ge(z_read, tiles(it, panel, m) - ZB)
                    for k in range(KU):
                        kk = KU * half + k
                        if is_split(u0):
                            if h1_at is not None and m == 0:
                                pe.wait_ge(h1_ready, it * (KT * BODY) + (h1_at + kk + 1))
                            last = products(z, whi[:, slot, k, cols], wlo[:, slot, k, cols], a_hi[:, kk, :],
                                            a_lo[:, kk, :], kk == 0, kk == KT - 1)
                        else:
                            if m == 0:
                                pe.wait_ge(z_read, tiles(it, panel - 2 + kk // MT, kk % MT))
                            last = nc.tensor.matmul(z, wraw[:, u0 % RAW, k, cols], h1[:, kk, :], start=(kk == 0),
                                                    stop=(kk == KT - 1))
                    if half == 1:
                        last.then_inc(z_ready, 1)
                if half == 0:
                    last.then_inc(half_used, 1)

            def turn_scores(b, r):
                n = b * BLOCK_ROUNDS + (r + 1)
                pe.wait_ge(mask_ready, n)
                nc.tensor.transpose(soft_ps[0:ROUND_TILES, 0:P], masked[:, r % 2, :], ident[:, :]).then_inc(scores_turned, 1)

            def turn_probs(b, r):
                n = b * BLOCK_ROUNDS + (r + 1)
                pe.wait_ge(prob_ready, n)
                nc.tensor.transpose(soft_ps[:, P:2 * P], prob[:, :, :].rearrange("t h l -> t (h l)"),
                                    ident[:, :]).then_inc(prob_turned, 1)

            def add_features(b, r):
                pe.wait_ge(pwin_ready, b * BLOCK_ROUNDS + (r + 1))
                for i in range(2):
                    at = WIN - (4 * r + 2 * i)
                    for half in range(2):
                        for j in range(CG):
                            last = nc.tensor.matmul(feat_ps[32 * j:32 * j + 32, half, 0:DM // 2],
                                                    pwin[:, 2 * j + i, at:at + 32],
                                                    xring[:, r % RING_ROUNDS, j, i, DM // 2 * half:DM // 2 * (half + 1)],
                                                    start=(r == 0 and i == 0), stop=(r == BLOCK_ROUNDS - 1 and i == 1),
                                                    tile_position=(0, 32 * j))
                last.then_inc(feat_added, 1)

            def block_end(b, it, c):
                pe.wait_ge(rows_a, b + 1)
                pe.wait_ge(rows_b, b + 1)
                for g in range(2):
                    if g:
                        pe.wait_ge(turned_read, it * 2 + (FEAT_READ[c] + 1))
                    elif c:
                        pe.wait_ge(gated_ready, it * BODY + BODY)
                    for k in range(KU):
                        last = nc.tensor.transpose(turn_ps[:, P * k:P * k + P], rows[:, KU * g + k:DM:KT], ident[:, :])
                    last.then_inc(turned, 1)

            def gate_broadcast(it, q, c):
                nc.tensor.matmul(gate_bc, ones[:, :], gate_e, start=True, stop=True).then_inc(gate_bc_ready, 1)

            def slots(c, it, xb, experts):
                for s in range(BU):
                    q, k = divmod(s, EU)
                    if experts:
                        if k == 4:
                            n = E * c + q
                            pe.wait_ge(gate_e_ready, it * BODY + (n + 1))
                            if n:
                                pe.wait_ge(gated_ready, it * BODY + n)
                        if k < 4:
                            unit(it, EXP0[c] + s, feat_hi[:, c, :, :], feat_lo[:, c, :, :])
                        else:
                            unit(it, EXP0[c] + s, h1_hi, h1_lo, KT * q)
                        if k == 4:
                            gate_broadcast(it, q, c)
                    if xb is not None:
                        r, third, _ = x_slots(s)
                        if third == 0 and r >= 1:
                            turn_scores(xb, r - 1)
                        if third == 1 and r >= 2:
                            add_features(xb, r - 2)
                        if third == 2 and r >= 1:
                            turn_probs(xb, r - 1)
                if xb is not None:
                    turn_scores(xb, BLOCK_ROUNDS - 1)
                    add_features(xb, BLOCK_ROUNDS - 2)
                    turn_probs(xb, BLOCK_ROUNDS - 1)
                    add_features(xb, BLOCK_ROUNDS - 1)

            def gate_logits(c, head):
                panel = GATE0[c] // 2 + head
                pe.wait_ge(z_read, tiles(0, panel, MT - 1))
                if head == 0 and not c:
                    pe.wait_ge(params_ready, 1)
                if head == 0 and c:
                    pe.wait_ge(omax_ready, c)
                for m in range(HT):
                    last = nc.tensor.matmul(logit_ps[32 * head:32 * head + E, :], gW2_sb[:, HT * head + m, :],
                                            h2[:, m, :], start=(m == 0), stop=(m == HT - 1),
                                            tile_position=(0, 32 * head))
                last.then_inc(logits_ready, 1)

            def head_logits(c):
                pe.wait_ge(rep_added, E * (c + 1))
                pe.wait_ge(gl_ready, c + 1)
                for b in range(CB):
                    for m in range(HT):
                        last = nc.tensor.matmul(logit_ps[:, 8 * b:8 * b + 2 * H], rep[:, m, P * b:P * b + P],
                                                hW_sb[:, m, :, :].rearrange("p h c -> p (h c)"), start=(m == 0),
                                                stop=(m == HT - 1))
                last.then_inc(out_logits, 1)

            def gate_stage(c):
                pe.wait_ge(turned_read, FEAT_READ[c] + 2 * CB)
                for n in range(GU):
                    unit(0, GATE0[c] + n, feat_hi[:, c, :, :], feat_lo[:, c, :, :])
                    if c and n == 1:
                        head_logits(c - 1)
                    if n % 2 and n > 1:
                        gate_logits(c, n // 2 - 1)
                gate_logits(c, H - 1)
                pe.wait_ge(gl_ready, c + 1)
                for b in range(CB):
                    last = nc.tensor.transpose(turn_ps[:, P * b:P * b + P], glogit[:, P * b:P * b + P], ident[:, :])
                last.then_inc(turned, 1)
                pe.wait_ge(gate_ready, c + 1)
                for b in range(CB):
                    last = nc.tensor.transpose(turn_ps[0:E, P * b:P * b + P], gate[:, b, :], ident[:, :])
                last.then_inc(turned, 1)

            pe.wait_ge(ident_ready, 1)
            with pe.Fori(0, CB) as it:
                slots(0, it, it, False)
                block_end(it, it, 0)
            pe.wait_ge(setup_loaded, 16 * 14)
            pe.wait_ge(turned_read, PRM_TURN)
            for a, n in ((0, 2 * N1 + N2), (1, N1 + 2 * N2 + H * HT)):
                last = nc.tensor.transpose(turn_ps[:, P * a:P * a + n], prm_rows[0:n, a, :], ident[0:n, 0:n])
            last.then_inc(turned, 1)
            gate_stage(0)
            with pe.Fori(0, ITERS) as it:
                slots(0, it, it + CB, True)
                block_end(it + CB, it, 1)
            gate_stage(1)
            with pe.Fori(0, ITERS) as it:
                slots(1, it, None, True)
            head_logits(1)


_INS = ["r_x", "r_D"] + ["L0_rec_" + n for n in ("aw", "gW1", "gb1", "gW2", "gb2", "eW1", "eb1", "bn1_g", "bn1_b",
                                                 "eW2", "eb2", "bn2_g", "bn2_b", "hW", "hb")]
_OUTS = [((512, 2), "float32")]


def kernel(**inputs):
    import numpy as _np
    import concourse.bacc as _bacc
    from concourse import mybir as _mybir
    from concourse.bass_utils import run_bass_kernel_spmd as _run

    nc = _bacc.Bacc("TRN2", target_bir_lowering=False, num_devices=1)
    arrays, args = {}, []
    for name in _INS:
        a = _np.ascontiguousarray(inputs[name])
        arrays[f"in_{name}_dram"] = a
        args.append(nc.dram_tensor(f"in_{name}_dram", a.shape, _mybir.dt.from_np(a.dtype), kind="ExternalInput").ap())
    for i, (shape, dtype) in enumerate(_OUTS):
        dt = _mybir.dt.from_np(_np.dtype(dtype))
        args.append(nc.dram_tensor(f"out_{i}_dram", shape, dt, kind="ExternalOutput").ap())
    rec_kernel(nc, *args)
    r = _run(nc, [arrays], core_ids=[0])
    return r.results[0]["out_0_dram"]
```

```python
from contextlib import ExitStack

import concourse.bass as bass
from concourse import mybir

F32 = mybir.dt.float32
F32R = mybir.dt.float32r
BF16 = mybir.dt.bfloat16
I32 = mybir.dt.int32
ALU = mybir.AluOpType
ACT = mybir.ActivationFunctionType
AX = mybir.AxisListType

P = 128
EPS = 1e-05
BN_SCALE = float((1.0 + EPS) ** -0.5)

CHUNK = 256
CG = 4
ROUND_TILES = 8
RING_ROUNDS = 4
BLOCK_ROUNDS = 8
RAW = 4
SPLIT = 3
AHEAD = 2
KU = 3
MT = 3
UNIT_COLS = MT * P
WIN = 30
ZB = 4
IN_FLIGHT = 2
BODY = 4
EU = 6


def rec_kernel(nc, x, D, aw, gW1, gb1, gW2, gb2, eW1, eb1, bn1_g, bn1_b, eW2, eb2, bn2_g, bn2_b, hW, hb, out):
    B, L, DM = x.shape
    H, _, HD = gW1.shape
    E = eW1.shape[0]
    KT = DM // P
    HT = HD // P
    NCH = B // CHUNK
    CB = CHUNK // P
    NBLK = B // P
    GU = 2 * H
    UNITS = GU + EU * E
    BU = BODY * EU
    ITERS = E // BODY
    assert 2 * L == P and KT == 2 * KU and HD == UNIT_COLS and ITERS == CB
    assert MT * (UNITS // 2) % ZB == 0 and MT * (BU // 2) % ZB == 0
    assert GU % RAW == 0 and BU % RAW == 0 and BU % SPLIT == 0

    x_v = x.rearrange("(b j r i h) l d -> b r (h l) j i d", j=CG, r=BLOCK_ROUNDS, i=2, h=2)
    gW1_v = gW1.rearrange("h (p k) n -> h p k n", k=KT)
    eW1_v = eW1.rearrange("e (p k) n -> e p k n", k=KT)
    eW2_v = eW2.rearrange("e (k p) n -> e p k n", p=P)

    with ExitStack() as ctx:
        def sb(name, shape, dt=F32):
            return ctx.enter_context(nc.sbuf_tensor(name, shape, dt))

        def psum(name, shape):
            return ctx.enter_context(nc.psum_tensor(name, shape, F32))

        def sem(name):
            return ctx.enter_context(nc.semaphore(name))

        xring = sb("xring", [P, RING_ROUNDS, CG, 2, DM])
        aw_bc = sb("aw_bc", [P, DM])
        prod_out = sb("prod_out", [P, 2, DM], BF16)
        copy_out = sb("copy_out", [P, 2, DM], BF16)
        score = sb("score", [P, 2, ROUND_TILES])
        rowsum = sb("rowsum", [P, 2, ROUND_TILES])
        penalty = sb("penalty", [P, ROUND_TILES])
        masked = sb("masked", [P, 2, ROUND_TILES])
        neg_max = sb("neg_max", [ROUND_TILES, 2, 2])
        expsum = sb("expsum", [ROUND_TILES, 2])
        recip = sb("recip", [ROUND_TILES, 2])
        prob = sb("prob", [P, 2, L])
        pwin = sb("pwin", [P, ROUND_TILES, WIN + 32])
        rows = sb("rows", [P, DM])
        feat_hi = sb("feat_hi", [P, NCH, KT, CHUNK], F32R)
        feat_lo = sb("feat_lo", [P, NCH, KT, CHUNK], F32R)
        ident = sb("ident", [P, P])
        wraw = sb("wraw", [P, RAW, KU, UNIT_COLS])
        whi = sb("whi", [P, SPLIT, KU, UNIT_COLS], F32R)
        wlo = sb("wlo", [P, SPLIT, KU, UNIT_COLS], F32R)
        h1 = sb("h1", [P, KT, CHUNK])
        with nc.sbuf_tensor("w2raw", [P, 2, KU, UNIT_COLS], F32) as w2raw:
            pass
        h1_hi = sb("h1_hi", [P, KT, CHUNK], F32R)
        h1_lo = sb("h1_lo", [P, KT, CHUNK], F32R)
        h2 = sb("h2", [P, HT, CHUNK])
        rep = sb("rep", [P, HT, CHUNK])
        gW2_sb = sb("gW2_sb", [P, H * HT, E])
        hW_sb = sb("hW_sb", [P, H * HT, 2])
        gb2_bc = sb("gb2_bc", [P, H, E])
        hb_bc = sb("hb_bc", [P, H, 2])
        head_is = sb("head_is", [P, NBLK, H])
        pick = sb("pick", [E, P])
        gl = sb("gl", [P, CB, E])
        gmax = sb("gmax", [P, CB])
        gexp = sb("gexp", [P, CB, E])
        gsum = sb("gsum", [P, CB])
        grec = sb("grec", [P, CB])
        gate = sb("gate", [P, CB, E])
        gateT = sb("gateT", [E, CHUNK])
        osel = sb("osel", [P, 2, H, 2])
        ol = sb("ol", [P, CB, 2])
        omax = sb("omax", [P, CB])
        oexp = sb("oexp", [P, CB, 2])
        osum = sb("osum", [P, CB])
        orec = sb("orec", [P, CB])
        out_sb = sb("out_sb", [P, NBLK, 2])
        scale = sb("scale", [P, E * (KT + HT)])
        bias = sb("bias", [P, E * (KT + HT) + H * HT])
        hW_m = hW_sb[:, :, :].rearrange("p (h m) c -> p m h c", h=H)
        w2_flat = w2raw[0:H * HT, :, :, :].rearrange("r a k n -> r (a k n)")
        gW2_rows, hW_rows = w2_flat[:, 0:P * E], w2_flat[:, P * E:P * (E + 2)]
        D_i, D_f = (w2_flat[0:NBLK, P * (E + n):P * (E + n + 1)] for n in (2, 3))
        prm = rows[:, 0:2 * P].rearrange("p (a n) -> p a n", a=2)
        prm_rows = h2[:, 0, 0:2 * P].rearrange("p (a n) -> p a n", a=2)
        glogit = h2[:, 1, :]
        gsel = h2[:, 2, 0:CB * H * E].rearrange("p (b h e) -> p b h e", b=CB, h=H)

        feat_ps = psum("feat_ps", [P, 2, 512])
        z_ps = psum("z_ps", [P, ZB, 512])
        soft_ps = psum("soft_ps", [P, 512])
        exps = soft_ps[0:ROUND_TILES, 2 * P:3 * P].rearrange("t (h l) -> t h l", h=2)
        turn_ps = psum("turn_ps", [P, 512])
        logit_ps = turn_ps[:, CHUNK:2 * CHUNK]
        gate_bc = turn_ps[:, 0:CHUNK]

        aw_loaded = sem("aw_loaded")
        prm_loaded = sem("prm_loaded")
        D_ready = sem("D_ready")
        x_loaded = [[sem(f"x_loaded{r}_{j}") for j in range(CG)] for r in range(RING_ROUNDS)]
        w_loaded = [sem(f"w_loaded{s}") for s in range(RAW)]
        w2_loaded = [sem(f"w2_loaded{half}") for half in range(2)]
        ident_zero = sem("ident_zero")
        ident_ready = sem("ident_ready")
        zeroed = sem("zeroed")
        link_dve = sem("link_dve")
        params_ready = sem("params_ready")
        scored = sem("scored")
        summed = sem("summed")
        pen_ready = sem("pen_ready")
        mask_ready = sem("mask_ready")
        scores_turned = sem("scores_turned")
        max_ready = sem("max_ready")
        exp_ready = sem("exp_ready")
        recip_ready = sem("recip_ready")
        prob_ready = sem("prob_ready")
        prob_turned = sem("prob_turned")
        pwin_ready = sem("pwin_ready")
        feat_added = sem("feat_added")
        rows_a = sem("rows_a")
        rows_b = sem("rows_b")
        turned = sem("turned")
        turned_hi = sem("turned_hi")
        turned_read = sem("turned_read")
        hi_ready = sem("hi_ready")
        lo_ready = sem("lo_ready")
        half_used = sem("half_used")
        z_ready = sem("z_ready")
        z_read = sem("z_read")
        h1_hi_ready = sem("h1_hi_ready")
        h1_ready = sem("h1_ready")
        logits_ready = sem("logits_ready")
        gl_ready = sem("gl_ready")
        gmax_ready = sem("gmax_ready")
        gexp_ready = sem("gexp_ready")
        gate_ready = sem("gate_ready")
        gateT_ready = sem("gateT_ready")
        pick_ready = sem("pick_ready")
        gate_bc_ready = sem("gate_bc_ready")
        gated_ready = sem("gated_ready")
        rep_zeroed = sem("rep_zeroed")
        rep_added = sem("rep_added")
        out_logits = sem("out_logits")
        omax_ready = sem("omax_ready")
        oexp_ready = sem("oexp_ready")
        out_ready = sem("out_ready")
        stored = sem("stored")


        def tiles(it, panel, m):
            return it * (MT * BU // 2) + (MT * panel + m + 1)

        def wait_unit_used(eng, it, u0):
            if u0 % 2 == 0:
                eng.wait_ge(half_used, it * (BU // 2) + (u0 // 2 + 1))
            else:
                eng.wait_ge(z_ready, tiles(it, u0 // 2, MT - 1))

        def is_split(u0):
            c, n = divmod(u0, UNITS)
            return c > 0 or n < GU or (n - GU) % EU < EU - 2

        def splits(it, u0):
            c, n = divmod(u0, UNITS)
            if c == 0 and n >= GU:
                q, k = divmod(n - GU, EU)
                return it * ((EU - 2) * BODY) + (GU + (EU - 2) * q + k + 1)
            return it * BU + (u0 + 1 - min(c, 1) * 2 * E)

        def raw_slot(u0):
            return (splits(0, u0) - 1) % RAW

        def wait_loaded(eng, it, u0):
            if is_split(u0):
                eng.wait_ge(w_loaded[raw_slot(u0)],
                            it * (16 * BU // RAW) + 16 * ((splits(0, u0) - 1) // RAW + 1))
            else:
                q, k = divmod(u0 - GU, EU)
                eng.wait_ge(w2_loaded[k % 2], 16 * (q + 1))

        N1, N2 = E * KT, E * HT
        GATE0 = [UNITS * c for c in range(NCH)]
        EXP0 = [UNITS * c + GU for c in range(NCH)]
        FEAT_TURN = [(2 * CB + 2) * c + (c > 0) for c in range(NCH)]
        PRM_TURN = 2 * CB
        GW2_AT = 2 * P
        HW_AT = GW2_AT + H * HT * E
        D_AT = HW_AT + H * HT * 2
        GATE_TURN = [FEAT_TURN[c] + 2 * CB + (c == 0) for c in range(NCH)]
        def turned_feat(c, g):
            dst = turn_ps if c else z_ps[:, g, :]
            return dst[:, 0:KU * P]

        FEAT_READ = [2 * CB * c + (c > 0) for c in range(NCH)]

        SCORES, BLOCK_THIRDS = 3, 3 * BLOCK_ROUNDS

        def to_score(third):
            return range(SCORES * third, min(SCORES * third + SCORES, ROUND_TILES))

        MASK_AT, MAX_AT, NORM_AT, PLACE_AT, EXP_AT = 0, 1, 3, 4, 3

        LEAD = 3
        LATE = 0
        SLOTS = UNITS + GU
        SLOT_THIRD = LEAD + BLOCK_THIRDS
        FIRST_SPREAD = BLOCK_ROUNDS
        ROUNDS = (1 + CB) * BLOCK_ROUNDS
        BLOCK_END = {3 * (BLOCK_ROUNDS * (j + 2) + 1) + 2 - SLOT_THIRD: j for j in range(CB)}
        BLOCK_GATED = [(t - GU) // EU for t in sorted(BLOCK_END)]
        GATE_COPY, GATE_PICK, GATE_NORM, GATE_SET = GU + 1, GU + 2, GU + 3, GU + 4
        HEAD_LOGITS, HEAD_PICK, HEAD_NORM = UNITS + 1, UNITS + 2, UNITS + 4

        def slot_of(s):
            c, n = divmod(s, UNITS)
            return (c, n, None, None) if n < GU else (c, None, *divmod(n - GU, EU))

        block = ctx.enter_context(nc.Block())

        @block.sync
        def _(sp):
            def load_round(b, r, wait):
                if wait:
                    sp.wait_ge(feat_added, b * BLOCK_ROUNDS + (r + 1 - RING_ROUNDS))
                for j in range(CG):
                    rr, jj = divmod(r * CG + j - IN_FLIGHT, CG)
                    if (wait and j) or (rr >= 0 and not wait):
                        sp.wait_ge(x_loaded[rr % RING_ROUNDS][jj], b * 32 + 16 * (rr // RING_ROUNDS + 1))
                    sp.dma_start(xring[:, r % RING_ROUNDS, j, :, :],
                                 x_v[b, r, :, j, :, :]).then_inc(x_loaded[r % RING_ROUNDS][j], 16)

            for r in range(RING_ROUNDS):
                load_round(0, r, False)
            sp.wait_ge(zeroed, 1)
            for a, at, src in ((0, 0, eb1), (0, N1, bn1_g), (0, 2 * N1, eb2), (1, 0, bn1_b), (1, N1, bn2_g),
                               (1, N1 + N2, bn2_b), (1, N1 + 2 * N2, gb1)):
                src = src.rearrange("e (m p) -> (e m) p", p=P)
                sp.dma_start(prm_rows[at:at + src.shape[0], a, :], src).then_inc(prm_loaded, 16)
            sp.dma_start(D_i.bitcast(I32), D.rearrange("(b p) -> b p", p=P)).then_inc(prm_loaded, 16)
            sp.dma_start(gW2_rows, gW2.rearrange("h (m p) e -> (h m) (p e)", p=P)).then_inc(prm_loaded, 16)
            sp.dma_start(hW_rows, hW.rearrange("h (m p) c -> (h m) (p c)", p=P)).then_inc(prm_loaded, 16)
            sp.dma_start(gb2_bc[:, :, :], gb2.partition_broadcast(P)).then_inc(prm_loaded, 16)
            sp.dma_start(hb_bc[:, :, :], hb.partition_broadcast(P)).then_inc(prm_loaded, 16)
            for r in range(RING_ROUNDS, BLOCK_ROUNDS):
                load_round(0, r, True)
            with sp.Fori(1, NBLK) as b:
                for r in range(BLOCK_ROUNDS):
                    load_round(b, r, True)
            sp.wait_ge(out_ready, NCH)
            sp.dma_start(out.rearrange("(b p) c -> p b c", p=P), out_sb[:, :, :]).then_inc(stored, 16)
            sp.wait_ge(stored, 16)

        @block.gpsimd
        def _(pool):
            nc.gpsimd.memset(ident[:, :], 0.0).then_inc(ident_zero, 1)
            pool.wait_ge(ident_zero, 1)
            nc.gpsimd.affine_select(out=ident[:, :], in_=ident[:, :], compare_op=ALU.not_equal, fill=1.0,
                                    base=0, pattern=[[-1, P]], channel_multiplier=1).then_inc(ident_ready, 1)

            def load_unit(it, u0, src):
                if is_split(u0):
                    if u0 >= RAW:
                        pool.wait_ge(lo_ready, splits(it, u0) - RAW)
                    pool.dma_start(wraw[:, raw_slot(u0), :, :], src).then_inc(w_loaded[raw_slot(u0)], 16)
                else:
                    wait_unit_used(pool, it, u0 - EU)
                    pool.dma_start(w2raw[:, u0 % 2, :, :], src).then_inc(w2_loaded[u0 % 2], 16)

            def gate_unit(u0, n):
                head, half = divmod(n, 2)
                load_unit(0, u0, gW1_v[head, :, KU * half:KU * half + KU, :])

            for late, at in ((False, 0), (True, CB * BLOCK_ROUNDS - LATE)):
                pool.wait_ge(x_loaded[at % RING_ROUNDS][CG - 1], 16 * (at // RING_ROUNDS + 1))
                for n in range(AHEAD, RAW) if late else range(AHEAD):
                    gate_unit(n, n)
            for c in range(NCH):
                for n in range(RAW if c == 0 else 0, GU):
                    gate_unit(GATE0[c] + n, n)
                with pool.Fori(0, ITERS) as it:
                    for n in range(BU):
                        q, k = divmod(n, EU)
                        panel, half = divmod(k, 2)
                        ks = slice(KU * half, KU * half + KU)
                        if panel < 2:
                            src = eW1_v[it * BODY + q, :, ks, UNIT_COLS * panel:UNIT_COLS * (panel + 1)]
                        else:
                            src = eW2_v[it * BODY + q, :, ks, :]
                        load_unit(it, EXP0[c] + n, src)
            for n in range(AHEAD):
                gate_unit(NCH * UNITS + n, n)
            for n in range(AHEAD):
                wait_loaded(pool, 0, NCH * UNITS + n)

        @block.scalar
        def _(act):
            act.dma_start(aw_bc[:, :], aw.partition_broadcast(P)).then_inc(aw_loaded, 16)

            def split_hi(it, u0):
                if not is_split(u0):
                    return
                wait_loaded(act, it, u0)
                if u0 >= SPLIT:
                    wait_unit_used(act, it, u0 - SPLIT)
                nc.scalar.activation(whi[:, u0 % SPLIT, :, :], wraw[:, raw_slot(u0), :, :], ACT.Copy).then_inc(hi_ready, 1)

            def sum_rows(b, r, ts):
                for t in ts:
                    j, i = divmod(t, 2)
                    if i == 0:
                        act.wait_ge(x_loaded[r % RING_ROUNDS][j], b * 32 + 16 * (r // RING_ROUNDS + 1))
                    at = r * ROUND_TILES + t
                    if at >= 2:
                        act.wait_ge(summed, b * (BLOCK_ROUNDS * ROUND_TILES) + (at - 1))
                    if t == 0 and r >= 2:
                        act.wait_ge(mask_ready, b * BLOCK_ROUNDS + (r - 1))
                    nc.scalar.activation(copy_out[:, t % 2, :], xring[:, r % RING_ROUNDS, j, i, :], ACT.Copy,
                                         accum_out=rowsum[:, r % 2, t:t + 1]).then_inc(summed, 1)

            def softmax_exp(b, r):
                act.wait_ge(max_ready, b * BLOCK_ROUNDS + (r + 1))
                for h in range(2):
                    last = nc.scalar.activation(exps[:, h, :], soft_ps[0:ROUND_TILES, L * h:L * h + L], ACT.Exp,
                                                bias=neg_max[:, r % 2, h:h + 1], accum_out=expsum[:, h:h + 1])
                last.then_inc(exp_ready, 1)

            def copy_rows(b):
                act.wait_ge(feat_added, b * BLOCK_ROUNDS + BLOCK_ROUNDS)
                nc.scalar.activation(rows[:, 0:DM // 2], feat_ps[:, 0, 0:DM // 2], ACT.Copy).then_inc(rows_a, 1)

            def features_hi(it, c, j, g, blk):
                act.wait_ge(turned, it * 2 + (FEAT_TURN[c] + 2 * j + g + 1))
                nc.scalar.activation(feat_hi[:, c, KU * g:KU * g + KU, blk],
                                     turned_feat(c, g).rearrange("p (k n) -> p k n", k=KU),
                                     ACT.Copy).then_inc(turned_hi, 1)

            def read_h1(it, q, panel0, c, ms):
                panel = EXP0[c] // 2 + 3 * q + panel0
                for m in ms:
                    t = MT * panel0 + m
                    act.wait_ge(z_ready, tiles(it, panel, m))
                    if c and q:
                        act.wait_ge(h1_ready, it * (KT * BODY) + (KT * (q - 1) + t + 1))
                    col = bass.ds(it * (KT * BODY) + (KT * q + t), 1)
                    nc.scalar.activation(h1[:, t, :], z_ps[:, (MT * panel + m) % ZB, 0:CHUNK], ACT.Relu,
                                         bias=bias[:, col], scale=scale[:, col]).then_inc(z_read, 1)

            def read_h2(it, q, c, ms):
                panel = EXP0[c] // 2 + 3 * q + 2
                if ms[0] == 0:
                    if c or q:
                        act.wait_ge(rep_added, it * BODY + (E * c + q))
                    else:
                        act.wait_ge(logits_ready, H)
                for m in ms:
                    act.wait_ge(z_ready, tiles(it, panel, m))
                    col = bass.ds(it * (HT * BODY) + (E * KT + HT * q + m), 1)
                    nc.scalar.activation(h2[:, m, :], z_ps[:, (MT * panel + m) % ZB, 0:CHUNK], ACT.Relu,
                                         bias=bias[:, col], scale=scale[:, col]).then_inc(z_read, 1)

            def read_gate(c, head, ms):
                panel = GATE0[c] // 2 + head
                if ms[0]:
                    pass
                elif head:
                    act.wait_ge(logits_ready, H * c + head)
                elif c:
                    act.wait_ge(rep_added, E * c)
                else:
                    act.wait_ge(params_ready, 1)
                for m in ms:
                    act.wait_ge(z_ready, tiles(0, panel, m))
                    at = N1 + N2 + HT * head + m
                    nc.scalar.activation(h2[:, m, :], z_ps[:, (MT * panel + m) % ZB, 0:CHUNK], ACT.Relu,
                                         bias=bias[:, at:at + 1]).then_inc(z_read, 1)

            def gate_exp(c):
                act.wait_ge(gmax_ready, c + 1)
                for b in range(CB):
                    last = nc.scalar.activation(gexp[:, b, :], gl[:, b, :], ACT.Exp, bias=gmax[:, b:b + 1],
                                                accum_out=gsum[:, b:b + 1])
                last.then_inc(gexp_ready, 1)

            def head_exp(c):
                act.wait_ge(omax_ready, c + 1)
                for b in range(CB):
                    last = nc.scalar.activation(oexp[:, b, :], ol[:, b, :], ACT.Exp, bias=omax[:, b:b + 1],
                                                accum_out=osum[:, b:b + 1])
                last.then_inc(oexp_ready, 1)

            def expert_reads(it, c, q, k, late):
                if k in (1, 3) and not late:
                    read_h1(it, q, k // 2, c, (0, 1))
                if k in (2, 4) and late:
                    read_h1(it, q, k // 2 - 1, c, (2,))
                if k == 5 and not late:
                    read_h2(it, q, c, (0, 1))
                if k == 0 and q and late:
                    read_h2(it, q - 1, c, (2,))

            def x_third(b, w):
                r, third = divmod(w, 3)
                if r < ROUNDS:
                    sum_rows(b, r, to_score(third))
                if third == 1 and 1 <= r <= ROUNDS:
                    softmax_exp(b, r - 1)

            def x_round(b, r):
                sum_rows(b, r, range(EXP_AT))
                softmax_exp(b, r - 1)
                sum_rows(b, r, range(EXP_AT, ROUND_TILES))

            for w in range(LEAD):
                x_third(0, w)
            for n in range(AHEAD):
                split_hi(0, n)
            with act.Fori(0, CB) as it:
                for r in range(1, BLOCK_ROUNDS + 1):
                    x_round(it, r)
                copy_rows(it)
                for g in range(2):
                    features_hi(it, 0, 0, g, bass.ds(it * P, P))
            for s in range(SLOTS):
                c, n, q, k = slot_of(s)
                split_hi(0, s + AHEAD)
                if n is not None and n >= 2 and n % 2 == 0:
                    read_gate(c, n // 2 - 1, (2,))
                elif k == 0 and q == 0:
                    read_gate(c, H - 1, (2,))
                elif n == 0 and c:
                    read_h2(0, E - 1, c - 1, (2,))
                elif k is not None:
                    expert_reads(0, c, q, k, True)
                if s in BLOCK_END:
                    copy_rows(CB + BLOCK_END[s])
                for g in range(2):
                    if s - 1 - g in BLOCK_END:
                        j = BLOCK_END[s - 1 - g]
                        features_hi(0, 1, j, g, slice(P * j, P * j + P))
                x_third(CB - 1, SLOT_THIRD + s)
                if s == GATE_NORM:
                    gate_exp(0)
                if s == HEAD_NORM:
                    head_exp(0)
                if n is not None and n % 2:
                    read_gate(c, n // 2, (0, 1))
                elif k is not None:
                    expert_reads(0, c, q, k, False)
            read_gate(1, H - 1, (2,))
            gate_exp(1)
            with act.Fori(0, ITERS) as it:
                for n in range(BU):
                    q, k = divmod(n, EU)
                    expert_reads(it, 1, q, k, True)
                    split_hi(it, EXP0[1] + n + AHEAD)
                    expert_reads(it, 1, q, k, False)
                read_h2(it, BODY - 1, 1, (2,))
            head_exp(1)

        @block.vector
        def _(dve):
            links = [0]

            def link(ins):
                links[0] += 1
                ins.then_inc(link_dve, 1)
                dve.wait_ge(link_dve, links[0])

            nc.vector.memset(h2[:, :, :], 0.0).then_inc(zeroed, 1)
            nc.vector.memset(pwin[:, :, :], 0.0)
            nc.vector.memset(prob[:, :, :], 0.0)
            nc.vector.memset(rep[:, :, :], 0.0).then_inc(rep_zeroed, 1)

            def split_lo(it, u0):
                if not is_split(u0):
                    return
                dve.wait_ge(hi_ready, splits(it, u0))
                nc.vector.tensor_tensor(wlo[:, u0 % SPLIT, :, :], wraw[:, raw_slot(u0), :, :],
                                        whi[:, u0 % SPLIT, :, :].bitcast(F32), ALU.subtract).then_inc(lo_ready, 1)

            def score_tile(b, r, t):
                j, i = divmod(t, 2)
                if i == 0:
                    dve.wait_ge(x_loaded[r % RING_ROUNDS][j], b * 32 + 16 * (r // RING_ROUNDS + 1))
                at = r * ROUND_TILES + t
                if at >= 2:
                    dve.wait_ge(scored, b * (BLOCK_ROUNDS * ROUND_TILES) + (at - 1))
                nc.vector.tensor_tensor_reduce(
                    out=prod_out[:, t % 2, :], in0=xring[:, r % RING_ROUNDS, j, i, :], in1=aw_bc[:, :], scale=1.0,
                    scalar=0.0, op0=ALU.mult, op1=ALU.add, accum_out=score[:, r % 2, t:t + 1]).then_inc(scored, 1)

            def mask_scores(b, r):
                n = b * BLOCK_ROUNDS + (r + 1)
                dve.wait_ge(summed, n * ROUND_TILES)
                nc.vector.tensor_scalar(penalty[:, :], rowsum[:, r % 2, :], 0.0, -3e38, ALU.is_equal,
                                        ALU.mult).then_inc(pen_ready, 1)
                dve.wait_ge(pen_ready, n)
                dve.wait_ge(scored, n * ROUND_TILES)
                nc.vector.scalar_tensor_tensor(out=masked[:, r % 2, :], in0=penalty[:, :], scalar=3.0,
                                               in1=score[:, r % 2, :], op0=ALU.mult,
                                               op1=ALU.add).then_inc(mask_ready, 1)

            def softmax_max(b, r):
                dve.wait_ge(scores_turned, b * BLOCK_ROUNDS + (r + 1))
                nc.vector.tensor_reduce(neg_max[:, r % 2, :],
                                        soft_ps[0:ROUND_TILES, 0:P].rearrange("t (h l) -> t h l", h=2),
                                        AX.X, ALU.max, negate=True).then_inc(max_ready, 1)

            def softmax_norm(b, r):
                n = b * BLOCK_ROUNDS + (r + 1)
                dve.wait_ge(exp_ready, n)
                nc.vector.reciprocal(recip[:, :], expsum[:, :]).then_inc(recip_ready, 1)
                dve.wait_ge(recip_ready, n)
                nc.vector.tensor_tensor(prob[0:ROUND_TILES, :, :], exps[:, :, :],
                                        recip[:, :].unsqueeze(2).to_broadcast([ROUND_TILES, 2, L]),
                                        ALU.mult).then_inc(prob_ready, 1)

            def place_probs(b, r):
                n = b * BLOCK_ROUNDS + r
                dve.wait_ge(prob_turned, n + 1)
                if r:
                    dve.wait_ge(feat_added, n)
                for h in range(2):
                    p = slice(L * h, L * h + L)
                    last = nc.vector.tensor_copy(pwin[p, :, WIN + h],
                                                 soft_ps[p, P:P + ROUND_TILES])
                last.then_inc(pwin_ready, 1)

            def copy_rows(b):
                dve.wait_ge(feat_added, b * BLOCK_ROUNDS + BLOCK_ROUNDS)
                nc.vector.tensor_copy(rows[:, DM // 2:DM], feat_ps[:, 1, 0:DM // 2]).then_inc(rows_b, 1)

            def features_lo(it, c, j, g, blk):
                dve.wait_ge(turned_hi, it * 2 + (2 * CB * c + 2 * j + g + 1))
                ks = slice(KU * g, KU * g + KU)
                nc.vector.tensor_tensor(feat_lo[:, c, ks, blk],
                                        turned_feat(c, g).rearrange("p (k n) -> p k n", k=KU),
                                        feat_hi[:, c, ks, blk].bitcast(F32),
                                        ALU.subtract).then_inc(turned_read, 1)

            def split_h1(it, q, panel0, c, m):
                panel = EXP0[c] // 2 + 3 * q + panel0
                t = MT * panel0 + m
                dve.wait_ge(z_read, tiles(it, panel, m))
                nc.vector.tensor_copy(h1_hi[:, t, :], h1[:, t, :]).then_inc(h1_hi_ready, 1)
                dve.wait_ge(h1_hi_ready, it * (KT * BODY) + (KT * q + t + 1))
                nc.vector.tensor_tensor(h1_lo[:, t, :], h1[:, t, :], h1_hi[:, t, :].bitcast(F32),
                                        ALU.subtract).then_inc(h1_ready, 1)

            def pick_gate(it, q, c):
                n = E * c + q
                if n:
                    dve.wait_ge(gate_bc_ready, it * BODY + n)
                nc.vector.tensor_copy(pick[:, :], ident[0:E, bass.ds(it * BODY + q, 1)].to_broadcast([E, P])
                                      ).then_inc(pick_ready, 1)

            def add_expert(it, q, c):
                n = E * c + q
                panel = EXP0[c] // 2 + 3 * q + 2
                dve.wait_ge(gate_bc_ready, it * BODY + (n + 1))
                if n:
                    dve.wait_ge(rep_added, it * BODY + n)
                dve.wait_ge(z_read, tiles(it, panel, MT - 1))
                nc.vector.tensor_tensor(h2[:, :, :], h2[:, :, :],
                                        gate_bc.unsqueeze(1).to_broadcast([P, HT, CHUNK]),
                                        ALU.mult).then_inc(gated_ready, 1)
                dve.wait_ge(gated_ready, it * BODY + (n + 1))
                nc.vector.tensor_tensor(rep[:, :, :], rep[:, :, :], h2[:, :, :], ALU.add).then_inc(rep_added, 1)

            def x_third(b, w, s=None):
                r, third = divmod(w, 3)
                scores = to_score(third) if r < ROUNDS else ()
                for t in scores[:1]:
                    score_tile(b, r, t)
                if third == 0 and FIRST_SPREAD <= r - 2 < ROUNDS:
                    place_probs(b, r - 2)
                if third == 0 and 1 <= r <= ROUNDS:
                    mask_scores(b, r - 1)
                if third == 1 and 1 <= r <= ROUNDS:
                    softmax_max(b, r - 1)
                if third == 2 and 1 <= r <= ROUNDS:
                    softmax_norm(b, r - 1)
                if s is not None:
                    split_lo(0, s + AHEAD)
                for t in scores[1:]:
                    score_tile(b, r, t)

            def x_round(b, r):
                for t in range(ROUND_TILES):
                    score_tile(b, r, t)
                    if t == MASK_AT:
                        mask_scores(b, r - 1)
                    if t == MAX_AT:
                        softmax_max(b, r - 1)
                    if t == NORM_AT:
                        softmax_norm(b, r - 1)
                    if t == PLACE_AT:
                        place_probs(b, r - 1)

            def head_pick(c):
                dve.wait_ge(out_logits, c + 1)
                for b in range(CB):
                    link(nc.vector.tensor_tensor(osel[:, b, :, :],
                                                 logit_ps[:, 8 * b:8 * b + 2 * H].rearrange("p (h c) -> p h c", c=2),
                                                 hb_bc[:, :, :], ALU.add))
                    link(nc.vector.tensor_tensor(osel[:, b, :, :], osel[:, b, :, :],
                                                 head_is[:, CB * c + b, :].unsqueeze(2).to_broadcast([P, H, 2]),
                                                 ALU.mult))
                    link(nc.vector.tensor_reduce(ol[:, b, :], osel[:, b, :, :].rearrange("p h c -> p c h"),
                                                 AX.X, ALU.add))
                nc.vector.tensor_reduce(omax[:, :], ol[:, :, :], AX.X, ALU.max, negate=True).then_inc(omax_ready, 1)

            def head_norm(c):
                dve.wait_ge(oexp_ready, c + 1)
                link(nc.vector.reciprocal(orec[:, :], osum[:, :]))
                nc.vector.tensor_tensor(out_sb[:, CB * c:CB * c + CB, :], oexp[:, :, :],
                                        orec[:, :].unsqueeze(2).to_broadcast([P, CB, 2]),
                                        ALU.mult).then_inc(out_ready, 1)

            def gate_copy(c):
                dve.wait_ge(logits_ready, H * (c + 1))
                for h in range(H):
                    rows_h = slice(32 * h, 32 * h + E)
                    last = nc.vector.tensor_copy(glogit[rows_h, :], logit_ps[rows_h, :])
                last.then_inc(gl_ready, 1)

            def gate_pick(c):
                dve.wait_ge(turned, GATE_TURN[c] + 1)
                for b in range(CB):
                    turned_b = turn_ps[:, P * b:P * b + P].rearrange("p (h e) -> p h e", h=H)
                    link(nc.vector.tensor_tensor(gsel[:, b, :, :], turned_b[:, :, 0:E], gb2_bc[:, :, :], ALU.add))
                    link(nc.vector.tensor_tensor(gsel[:, b, :, :], gsel[:, b, :, :],
                                                 head_is[:, CB * c + b, :].unsqueeze(2).to_broadcast([P, H, E]),
                                                 ALU.mult))
                    link(nc.vector.tensor_reduce(gl[:, b, :], gsel[:, b, :, :].rearrange("p h e -> p e h"),
                                                 AX.X, ALU.add))
                nc.vector.tensor_reduce(gmax[:, :], gl[:, :, :], AX.X, ALU.max, negate=True).then_inc(gmax_ready, 1)

            def gate_norm(c):
                dve.wait_ge(gexp_ready, c + 1)
                link(nc.vector.reciprocal(grec[:, :], gsum[:, :]))
                nc.vector.tensor_tensor(gate[:, :, :], gexp[:, :, :],
                                        grec[:, :].unsqueeze(2).to_broadcast([P, CB, E]),
                                        ALU.mult).then_inc(gate_ready, 1)

            def gate_set(c):
                dve.wait_ge(turned, GATE_TURN[c] + 2)
                nc.vector.tensor_copy(gateT[:, :], turn_ps[0:E, 0:CHUNK]).then_inc(gateT_ready, 1)
                dve.wait_ge(gateT_ready, c + 1)
                dve.wait_ge(rep_zeroed, c + 1)

            def set_params():
                dve.wait_ge(turned, PRM_TURN + 1)
                nc.vector.tensor_copy(gW2_sb[:, :, :],
                                      turn_ps[:, GW2_AT:HW_AT].rearrange("p (e r) -> p r e", e=E))
                nc.vector.tensor_copy(hW_sb[:, :, :], turn_ps[:, HW_AT:D_AT].rearrange("p (c r) -> p r c", c=2))
                for h in range(H):
                    nc.vector.tensor_scalar(head_is[:, :, h], turn_ps[:, D_AT:D_AT + NBLK], float(h), None,
                                            ALU.is_equal)
                nc.vector.tensor_copy(prm[:, 0, 0:2 * N1 + N2], turn_ps[:, 0:2 * N1 + N2])
                nc.vector.tensor_copy(prm[:, 1, 0:N1 + 2 * N2 + H * HT],
                                      turn_ps[:, P:P + N1 + 2 * N2 + H * HT]).then_inc(turned_read, 1)
                dve.wait_ge(turned_read, PRM_TURN + 1)
                nc.vector.tensor_scalar(scale[:, 0:N1], prm[:, 0, N1:2 * N1], BN_SCALE, None, ALU.mult)
                link(nc.vector.tensor_scalar(scale[:, N1:N1 + N2], prm[:, 1, N1:N1 + N2], BN_SCALE, None, ALU.mult))
                nc.vector.tensor_tensor(bias[:, 0:N1], prm[:, 0, 0:N1], scale[:, 0:N1], ALU.mult)
                link(nc.vector.tensor_tensor(bias[:, N1:N1 + N2], prm[:, 0, 2 * N1:2 * N1 + N2], scale[:, N1:N1 + N2],
                                             ALU.mult))
                nc.vector.tensor_tensor(bias[:, 0:N1], bias[:, 0:N1], prm[:, 1, 0:N1], ALU.add)
                nc.vector.tensor_tensor(bias[:, N1:N1 + N2], bias[:, N1:N1 + N2],
                                        prm[:, 1, N1 + N2:N1 + 2 * N2], ALU.add)
                nc.vector.tensor_copy(bias[:, N1 + N2:N1 + N2 + H * HT],
                                      prm[:, 1, N1 + 2 * N2:N1 + 2 * N2 + H * HT]).then_inc(params_ready, 1)

            dve.wait_ge(aw_loaded, 16)
            for w in range(LEAD):
                x_third(0, w)
            for n in range(AHEAD):
                split_lo(0, n)
            with dve.Fori(0, CB) as it:
                for r in range(1, BLOCK_ROUNDS + 1):
                    x_round(it, r)
                copy_rows(it)
                for g in range(2):
                    features_lo(it, 0, 0, g, bass.ds(it * P, P))
            dve.wait_ge(prm_loaded, 16 * 12)
            nc.vector.tensor_copy(D_f, D_i.bitcast(I32)).then_inc(D_ready, 1)
            for s in range(SLOTS):
                c, n, q, k = slot_of(s)
                x_third(CB - 1, SLOT_THIRD + s, s)
                if s == 0:
                    set_params()
                if s in BLOCK_END:
                    copy_rows(CB + BLOCK_END[s])
                for g in range(2):
                    if s - 1 - g in BLOCK_END:
                        j = BLOCK_END[s - 1 - g]
                        features_lo(0, 1, j, g, slice(P * j, P * j + P))
                if k == 0 and q:
                    add_expert(0, q - 1, c)
                if n == 0 and c:
                    add_expert(0, E - 1, c - 1)
                if s == GATE_COPY:
                    gate_copy(0)
                if s == GATE_PICK:
                    gate_pick(0)
                if s == GATE_NORM:
                    gate_norm(0)
                if s == GATE_SET:
                    gate_set(0)
                if k == 4:
                    pick_gate(0, q, c)
                if s == HEAD_PICK:
                    head_pick(0)
                if s == HEAD_NORM:
                    head_norm(0)
                    nc.vector.memset(rep[:, :, :], 0.0).then_inc(rep_zeroed, 1)
            gate_copy(1)
            gate_pick(1)
            gate_norm(1)
            gate_set(1)
            with dve.Fori(0, ITERS) as it:
                for n in range(BU):
                    q, k = divmod(n, EU)
                    if k in (2, 4):
                        for m in range(MT):
                            split_h1(it, q, k // 2 - 1, 1, m)
                    split_lo(it, EXP0[1] + n + AHEAD)
                    if k == 4:
                        pick_gate(it, q, 1)
                    if k == 0 and q:
                        add_expert(it, q - 1, 1)
                add_expert(it, BODY - 1, 1)
            head_pick(1)
            head_norm(1)

        @block.tensor
        def _(pe):
            def products(psum_tile, w_hi, w_lo, a_hi, a_lo, first, last):
                nc.tensor.matmul(psum_tile, w_hi, a_hi, start=first, stop=False)
                nc.tensor.matmul(psum_tile, w_hi, a_lo, start=False, stop=False)
                return nc.tensor.matmul(psum_tile, w_lo, a_hi, start=False, stop=last)

            def unit(it, u0, a_hi, a_lo, h1_at=None):
                panel, half = divmod(u0, 2)
                slot = u0 % SPLIT
                if is_split(u0):
                    pe.wait_ge(lo_ready, splits(it, u0))
                else:
                    wait_loaded(pe, it, u0)
                for m in range(MT):
                    z = z_ps[:, (MT * panel + m) % ZB, 0:CHUNK]
                    cols = slice(P * m, P * m + P)
                    if half == 0 and MT * panel + m >= ZB:
                        pe.wait_ge(z_read, tiles(it, panel, m) - ZB)
                    for k in range(KU):
                        kk = KU * half + k
                        if is_split(u0):
                            if h1_at is not None and m == 0:
                                pe.wait_ge(h1_ready, it * (KT * BODY) + (h1_at + kk + 1))
                            last = products(z, whi[:, slot, k, cols], wlo[:, slot, k, cols], a_hi[:, kk, :],
                                            a_lo[:, kk, :], kk == 0, kk == KT - 1)
                        else:
                            if m == 0:
                                pe.wait_ge(z_read, tiles(it, panel - 2 + kk // MT, kk % MT))
                            last = nc.tensor.matmul(z, w2raw[:, half, k, cols], h1[:, kk, :], start=(kk == 0),
                                                    stop=(kk == KT - 1))
                    if half == 1:
                        last.then_inc(z_ready, 1)
                if half == 0:
                    last.then_inc(half_used, 1)

            def turn_scores(b, r):
                n = b * BLOCK_ROUNDS + (r + 1)
                pe.wait_ge(mask_ready, n)
                nc.tensor.transpose(soft_ps[0:ROUND_TILES, 0:P], masked[:, r % 2, :], ident[:, :]).then_inc(scores_turned, 1)

            def turn_probs(b, r):
                n = b * BLOCK_ROUNDS + (r + 1)
                pe.wait_ge(prob_ready, n)
                nc.tensor.transpose(soft_ps[:, P:2 * P], prob[:, :, :].rearrange("t h l -> t (h l)"),
                                    ident[:, :]).then_inc(prob_turned, 1)

            def add_features(b, r, between=None):
                pe.wait_ge(pwin_ready, b * BLOCK_ROUNDS + (r + 1))
                in_block = r % BLOCK_ROUNDS
                if r and in_block == 0:
                    pe.wait_ge(rows_a, b + r // BLOCK_ROUNDS)
                    pe.wait_ge(rows_b, b + r // BLOCK_ROUNDS)
                for i in range(2):
                    if i and between is not None:
                        turn_scores(b, between)
                    at = WIN - (4 * in_block + 2 * i)
                    for half in range(2):
                        for j in range(CG):
                            last = nc.tensor.matmul(feat_ps[32 * j:32 * j + 32, half, 0:DM // 2],
                                                    pwin[:, 2 * j + i, at:at + 32],
                                                    xring[:, r % RING_ROUNDS, j, i, DM // 2 * half:DM // 2 * (half + 1)],
                                                    start=(in_block == 0 and i == 0),
                                                    stop=(in_block == BLOCK_ROUNDS - 1 and i == 1),
                                                    tile_position=(0, 32 * j))
                last.then_inc(feat_added, 1)

            def turn_features(b, it, c, j, g):
                if g == 0:
                    pe.wait_ge(rows_a, b + 1)
                    pe.wait_ge(rows_b, b + 1)
                    if c:
                        pe.wait_ge(gated_ready, BLOCK_GATED[j])
                elif c:
                    pe.wait_ge(turned_read, it * 2 + (FEAT_READ[c] + 2 * j + 1))
                for k in range(KU):
                    last = nc.tensor.transpose(turned_feat(c, g)[:, P * k:P * k + P], rows[:, KU * g + k:DM:KT], ident[:, :])
                last.then_inc(turned, 1)

            def gate_broadcast(it, q, c):
                n = E * c + q
                pe.wait_ge(pick_ready, it * BODY + (n + 1))
                if n:
                    pe.wait_ge(gated_ready, it * BODY + n)
                if c == 0:
                    done = sum(2 for t in BLOCK_END if GU + EU * q + 5 >= t)
                    if done:
                        pe.wait_ge(turned_read, FEAT_READ[1] + done)
                pe.wait_ge(params_ready, 1)
                nc.tensor.matmul(gate_bc, pick[:, :], gateT[:, :], start=True, stop=True).then_inc(gate_bc_ready, 1)

            def x_third(b, w):
                r, third = divmod(w, 3)
                if third == 0 and 1 <= r <= ROUNDS:
                    turn_scores(b, r - 1)
                if third == 1 and FIRST_SPREAD <= r - 2 < ROUNDS:
                    add_features(b, r - 2)
                if third == 2 and 1 <= r <= ROUNDS:
                    turn_probs(b, r - 1)

            def expert_unit(it, c, q, n):
                k = n % EU
                if k < 4:
                    unit(it, EXP0[c] + n, feat_hi[:, c, :, :], feat_lo[:, c, :, :])
                else:
                    unit(it, EXP0[c] + n, h1_hi, h1_lo, KT * q)
                if k == 5:
                    gate_broadcast(it, q, c)

            def gate_logits(c, head):
                panel = GATE0[c] // 2 + head
                pe.wait_ge(z_read, tiles(0, panel, MT - 1))
                if head == 0 and not c:
                    pe.wait_ge(params_ready, 1)
                if head == 0 and c:
                    pe.wait_ge(omax_ready, c)
                for m in range(HT):
                    last = nc.tensor.matmul(logit_ps[32 * head:32 * head + E, :], gW2_sb[:, HT * head + m, :],
                                            h2[:, m, :], start=(m == 0), stop=(m == HT - 1),
                                            tile_position=(0, 32 * head))
                last.then_inc(logits_ready, 1)

            def head_logits(c):
                pe.wait_ge(rep_added, E * (c + 1))
                pe.wait_ge(gl_ready, c + 1)
                for b in range(CB):
                    for m in range(HT):
                        last = nc.tensor.matmul(logit_ps[:, 8 * b:8 * b + 2 * H], rep[:, m, P * b:P * b + P],
                                                hW_m[:, m, :, :], start=(m == 0),
                                                stop=(m == HT - 1))
                last.then_inc(out_logits, 1)

            def turn_gate_logits(c):
                pe.wait_ge(gl_ready, c + 1)
                for b in range(CB):
                    last = nc.tensor.transpose(turn_ps[:, P * b:P * b + P], glogit[:, P * b:P * b + P], ident[:, :])
                last.then_inc(turned, 1)

            def turn_gate(c):
                pe.wait_ge(gate_ready, c + 1)
                for b in range(CB):
                    last = nc.tensor.transpose(turn_ps[0:E, P * b:P * b + P], gate[:, b, :], ident[:, :])
                last.then_inc(turned, 1)

            def turn_params():
                pe.wait_ge(prm_loaded, 16 * 12)
                pe.wait_ge(D_ready, 1)
                pe.wait_ge(turned_read, PRM_TURN)
                for a, n in ((0, 2 * N1 + N2), (1, N1 + 2 * N2 + H * HT)):
                    nc.tensor.transpose(turn_ps[:, P * a:P * a + n], prm_rows[0:n, a, :], ident[0:n, 0:n])
                n = H * HT
                for src, cols, at in ((gW2_rows, E, GW2_AT), (hW_rows, 2, HW_AT)):
                    for e in range(cols):
                        nc.tensor.transpose(turn_ps[:, at + n * e:at + n * e + n], src[:, e::cols], ident[0:n, 0:n])
                last = nc.tensor.transpose(turn_ps[:, D_AT:D_AT + NBLK], D_f, ident[0:NBLK, 0:NBLK])
                last.then_inc(turned, 1)

            pe.wait_ge(ident_ready, 1)
            with pe.Fori(0, CB) as it:
                turn_scores(it, 0)
                for r in range(BLOCK_ROUNDS):
                    turn_probs(it, r)
                    add_features(it, r, r + 1 if r < BLOCK_ROUNDS - 1 else None)
                for g in range(2):
                    turn_features(it, it, 0, 0, g)
            for s in range(SLOTS):
                c, n, q, k = slot_of(s)
                if n == 0:
                    pe.wait_ge(turned_read, FEAT_READ[c] + 2 * CB)
                if n is not None:
                    unit(0, s, feat_hi[:, c, :, :], feat_lo[:, c, :, :])
                    if s == 0:
                        turn_params()
                    if n >= 2 and n % 2 == 0:
                        gate_logits(c, n // 2 - 1)
                else:
                    expert_unit(0, c, q, s - EXP0[c])
                    if q == 0 and k == 0:
                        gate_logits(c, H - 1)
                if s == GATE_COPY:
                    turn_gate_logits(0)
                if s == GATE_NORM:
                    turn_gate(0)
                if s == HEAD_LOGITS:
                    head_logits(0)
                x_third(CB - 1, SLOT_THIRD + s)
                for g in range(2):
                    if s - g in BLOCK_END:
                        turn_features(CB + BLOCK_END[s - g], 0, 1, BLOCK_END[s - g], g)
            gate_logits(1, H - 1)
            turn_gate_logits(1)
            turn_gate(1)
            with pe.Fori(0, ITERS) as it:
                for n in range(BU):
                    expert_unit(it, 1, n // EU, n)
            head_logits(1)


_INS = ["r_x", "r_D"] + ["L0_rec_" + n for n in ("aw", "gW1", "gb1", "gW2", "gb2", "eW1", "eb1", "bn1_g", "bn1_b",
                                                 "eW2", "eb2", "bn2_g", "bn2_b", "hW", "hb")]
_OUTS = [((512, 2), "float32")]


def kernel(**inputs):
    import numpy as _np
    import concourse.bacc as _bacc
    from concourse import mybir as _mybir
    from concourse.bass_utils import run_bass_kernel_spmd as _run

    nc = _bacc.Bacc("TRN2", target_bir_lowering=False, num_devices=1)
    arrays, args = {}, []
    for name in _INS:
        a = _np.ascontiguousarray(inputs[name])
        arrays[f"in_{name}_dram"] = a
        args.append(nc.dram_tensor(f"in_{name}_dram", a.shape, _mybir.dt.from_np(a.dtype), kind="ExternalInput").ap())
    for i, (shape, dtype) in enumerate(_OUTS):
        dt = _mybir.dt.from_np(_np.dtype(dtype))
        args.append(nc.dram_tensor(f"out_{i}_dram", shape, dt, kind="ExternalOutput").ap())
    rec_kernel(nc, *args)
    r = _run(nc, [arrays], core_ids=[0])
    return r.results[0]["out_0_dram"]
```

```python
from contextlib import ExitStack

import concourse.bass as bass
from concourse import mybir

F32 = mybir.dt.float32
F32R = mybir.dt.float32r
BF16 = mybir.dt.bfloat16
I32 = mybir.dt.int32
ALU = mybir.AluOpType
ACT = mybir.ActivationFunctionType
AX = mybir.AxisListType

P = 128
EPS = 1e-05
BN_SCALE = float((1.0 + EPS) ** -0.5)

CHUNK = 256
CG = 4
ROUND_TILES = 8
RING_ROUNDS = 4
BLOCK_ROUNDS = 8
RAW = 4
SPLIT = 3
AHEAD = 2
KU = 3
MT = 3
UNIT_COLS = MT * P
WIN = 30
ZB = 4
IN_FLIGHT = 4
BODY = 4
EU = 6


def rec_kernel(nc, x, D, aw, gW1, gb1, gW2, gb2, eW1, eb1, bn1_g, bn1_b, eW2, eb2, bn2_g, bn2_b, hW, hb, out):
    B, L, DM = x.shape
    H, _, HD = gW1.shape
    E = eW1.shape[0]
    KT = DM // P
    HT = HD // P
    NCH = B // CHUNK
    CB = CHUNK // P
    NBLK = B // P
    GU = 2 * H
    BU = BODY * EU
    ITERS = E // BODY
    assert 2 * L == P and KT == 2 * KU and HD == UNIT_COLS and ITERS == CB
    assert MT * (NCH * GU + EU * E) // 2 % ZB == 0 and MT * (BU // 2) % ZB == 0
    assert GU % RAW == 0 and BU % RAW == 0 and BU % SPLIT == 0

    x_v = x.rearrange("(b j r i h) l d -> b r (h l) j i d", j=CG, r=BLOCK_ROUNDS, i=2, h=2)
    gW1_v = gW1.rearrange("h (p k) n -> h p k n", k=KT)
    eW1_v = eW1.rearrange("e (p k) n -> e p k n", k=KT)
    eW2_v = eW2.rearrange("e (k p) n -> e p k n", p=P)

    with ExitStack() as ctx:
        def sb(name, shape, dt=F32):
            return ctx.enter_context(nc.sbuf_tensor(name, shape, dt))

        def psum(name, shape):
            return ctx.enter_context(nc.psum_tensor(name, shape, F32))

        def sem(name):
            return ctx.enter_context(nc.semaphore(name))

        xring = sb("xring", [P, RING_ROUNDS, CG, 2, DM])
        aw_bc = sb("aw_bc", [P, DM])
        prod_out = sb("prod_out", [P, 2, DM], BF16)
        copy_out = sb("copy_out", [P, 2, DM], BF16)
        score = sb("score", [P, 2, ROUND_TILES])
        rowsum = sb("rowsum", [P, 2, ROUND_TILES])
        penalty = sb("penalty", [P, ROUND_TILES])
        masked = sb("masked", [P, 2, ROUND_TILES])
        neg_max = sb("neg_max", [ROUND_TILES, 2, 2])
        expsum = sb("expsum", [ROUND_TILES, 2])
        recip = sb("recip", [ROUND_TILES, 2])
        prob = sb("prob", [P, 2, L])
        pwin = sb("pwin", [P, ROUND_TILES, WIN + 32])
        rows = sb("rows", [P, DM])
        feat_hi = sb("feat_hi", [P, NCH, KT, CHUNK], F32R)
        feat_lo = sb("feat_lo", [P, NCH, KT, CHUNK], F32R)
        ident = sb("ident", [P, P])
        wraw = sb("wraw", [P, RAW, KU, UNIT_COLS])
        whi = sb("whi", [P, SPLIT, KU, UNIT_COLS], F32R)
        wlo = sb("wlo", [P, SPLIT, KU, UNIT_COLS], F32R)
        h1 = sb("h1", [P, KT, CHUNK])
        with nc.sbuf_tensor("w2raw", [P, 2, KU, UNIT_COLS], F32) as w2raw:
            pass
        h1_hi = sb("h1_hi", [P, KT, CHUNK], F32R)
        h1_lo = sb("h1_lo", [P, KT, CHUNK], F32R)
        h2 = sb("h2", [P, HT, CHUNK])
        rep = sb("rep", [P, HT, CHUNK])
        gW2_sb = sb("gW2_sb", [P, H * HT, E])
        hW_sb = sb("hW_sb", [P, H * HT, 2])
        gb2_bc = sb("gb2_bc", [P, H, E])
        hb_bc = sb("hb_bc", [P, H, 2])
        head_is = sb("head_is", [P, NBLK, H])
        pick = sb("pick", [E, P])
        gl = sb("gl", [P, CB, E])
        gmax = sb("gmax", [P, CB])
        gexp = sb("gexp", [P, CB, E])
        gsum = sb("gsum", [P, CB])
        grec = sb("grec", [P, CB])
        gate = sb("gate", [P, CB, E])
        gateT = sb("gateT", [E, CHUNK])
        osel = sb("osel", [P, 2, H, 2])
        ol = sb("ol", [P, CB, 2])
        omax = sb("omax", [P, CB])
        oexp = sb("oexp", [P, CB, 2])
        osum = sb("osum", [P, CB])
        orec = sb("orec", [P, CB])
        out_sb = sb("out_sb", [P, NBLK, 2])
        scale = sb("scale", [P, E * (KT + HT)])
        bias = sb("bias", [P, E * (KT + HT) + H * HT])
        hW_m = hW_sb[:, :, :].rearrange("p (h m) c -> p m h c", h=H)
        w2_flat = w2raw[0:H * HT, :, :, :].rearrange("r a k n -> r (a k n)")
        gW2_rows, hW_rows = w2_flat[:, 0:P * E], w2_flat[:, P * E:P * (E + 2)]
        D_i, D_f = (w2_flat[0:NBLK, P * (E + n):P * (E + n + 1)] for n in (2, 3))
        prm = rows[:, 0:2 * P].rearrange("p (a n) -> p a n", a=2)
        prm_rows = h2[:, 0, 0:2 * P].rearrange("p (a n) -> p a n", a=2)
        glogit = rows[:, 0:CHUNK]
        gsel = rows[:, CHUNK:CHUNK + CB * H * E].rearrange("p (b h e) -> p b h e", b=CB, h=H)

        feat_ps = psum("feat_ps", [P, 2, 512])
        z_ps = psum("z_ps", [P, ZB, 512])
        soft_ps = psum("soft_ps", [P, 512])
        exps = soft_ps[0:ROUND_TILES, 2 * P:3 * P].rearrange("t (h l) -> t h l", h=2)
        turn_ps = psum("turn_ps", [P, 512])
        logit_ps = turn_ps[:, CHUNK:2 * CHUNK]
        gate_bc = turn_ps[:, 0:CHUNK]

        aw_loaded = sem("aw_loaded")
        prm_loaded = sem("prm_loaded")
        D_ready = sem("D_ready")
        x_loaded = [[sem(f"x_loaded{r}_{j}") for j in range(CG)] for r in range(RING_ROUNDS)]
        w_loaded = [sem(f"w_loaded{s}") for s in range(RAW)]
        w2_loaded = [sem(f"w2_loaded{half}") for half in range(2)]
        ident_zero = sem("ident_zero")
        ident_ready = sem("ident_ready")
        zeroed = sem("zeroed")
        link_dve = sem("link_dve")
        params_ready = sem("params_ready")
        scored = sem("scored")
        summed = sem("summed")
        pen_ready = sem("pen_ready")
        mask_ready = sem("mask_ready")
        scores_turned = sem("scores_turned")
        max_ready = sem("max_ready")
        exp_ready = sem("exp_ready")
        recip_ready = sem("recip_ready")
        prob_ready = sem("prob_ready")
        prob_turned = sem("prob_turned")
        pwin_ready = sem("pwin_ready")
        feat_added = sem("feat_added")
        rows_a = sem("rows_a")
        rows_b = sem("rows_b")
        turned = sem("turned")
        turned_hi = sem("turned_hi")
        turned_read = sem("turned_read")
        hi_ready = sem("hi_ready")
        lo_ready = sem("lo_ready")
        half_used = sem("half_used")
        z_ready = sem("z_ready")
        z_read = sem("z_read")
        h1_hi_ready = sem("h1_hi_ready")
        h1_ready = sem("h1_ready")
        logits_ready = sem("logits_ready")
        gl_ready = sem("gl_ready")
        gmax_ready = sem("gmax_ready")
        gexp_ready = sem("gexp_ready")
        gate_ready = sem("gate_ready")
        gateT_ready = sem("gateT_ready")
        pick_ready = sem("pick_ready")
        gate_bc_ready = sem("gate_bc_ready")
        gated_ready = sem("gated_ready")
        rep_zeroed = sem("rep_zeroed")
        rep_added = sem("rep_added")
        out_logits = sem("out_logits")
        omax_ready = sem("omax_ready")
        oexp_ready = sem("oexp_ready")
        out_ready = sem("out_ready")
        stored = sem("stored")


        def tiles(it, panel, m):
            return it * (MT * BU // 2) + (MT * panel + m + 1)

        def wait_unit_used(eng, it, u0):
            if u0 % 2 == 0:
                eng.wait_ge(half_used, it * (BU // 2) + (u0 // 2 + 1))
            else:
                eng.wait_ge(z_ready, tiles(it, u0 // 2, MT - 1))

        GATES = [[(c, n, None, None) for n in range(GU)] for c in range(NCH)]
        EXPERTS = [[(0, None, q, k) for k in range(EU)] for q in range(E)]
        ORDER = (GATES[0] + [u for expert in EXPERTS[:-1] for u in expert] + EXPERTS[-1][:2] + GATES[1]
                 + EXPERTS[-1][2:])
        SLOTS = len(ORDER)

        def gate_at(c):
            return ORDER.index((c, 0, None, None))

        def expert_at(c, q, k):
            return SLOTS + EU * q + k if c else ORDER.index((0, None, q, k))

        SPLIT_FROM = 6

        def is_split(u0):
            if u0 >= SLOTS:
                return True
            _, n, q, k = ORDER[u0]
            return n is not None or k < EU - 2 or q >= SPLIT_FROM

        def splits(it, u0):
            return it * BU + sum(is_split(v) for v in range(u0 + 1))

        def h1_splits(it, c, q, t):
            return it * (KT * BODY) + (KT * (q + (E if c else 0) - SPLIT_FROM) + t + 1)

        def raw_slot(u0):
            return (splits(0, u0) - 1) % RAW

        def turned_gate(c):
            return (soft_ps if c else turn_ps)[0:E, 0:CHUNK]

        def wait_loaded(eng, it, u0):
            if is_split(u0):
                eng.wait_ge(w_loaded[raw_slot(u0)],
                            it * (16 * BU // RAW) + 16 * ((splits(0, u0) - 1) // RAW + 1))
            else:
                eng.wait_ge(w2_loaded[u0 % 2], 16 * (ORDER[u0][2] + 1))

        N1, N2 = E * KT, E * HT
        FEAT_TURN = [(2 * CB + 2) * c + (c > 0) for c in range(NCH)]
        PRM_TURN = 2 * CB
        GW2_AT = 2 * P
        HW_AT = GW2_AT + H * HT * E
        D_AT = HW_AT + H * HT * 2
        GATE_TURN = [FEAT_TURN[c] + 2 * CB + (c == 0) for c in range(NCH)]

        def turned_feat(c, j, g):
            if c == 0:
                return z_ps[:, g, 0:KU * P]
            return (soft_ps if (j, g) == (CB - 1, 1) else turn_ps)[:, 0:KU * P]

        FEAT_READ = [2 * CB * c + (c > 0) for c in range(NCH)]

        SCORES, BLOCK_THIRDS = 3, 3 * BLOCK_ROUNDS

        def to_score(third):
            return range(SCORES * third, min(SCORES * third + SCORES, ROUND_TILES))

        MASK_AT, MAX_AT, NORM_AT, PLACE_AT, EXP_AT = 0, 1, 3, 4, 3

        LEAD = 3
        SLOT_THIRD = LEAD + BLOCK_THIRDS
        FIRST_SPREAD = BLOCK_ROUNDS
        ROUNDS = (1 + CB) * BLOCK_ROUNDS
        BLOCK_END = {3 * (BLOCK_ROUNDS * (j + 2) + 1) + 2 - SLOT_THIRD: j for j in range(CB)}
        BLOCK_GATED = [(t - GU) // EU for t in sorted(BLOCK_END)]
        TURN_SLOT = {(j, g): t + (g if j == 0 else 0) for t, j in BLOCK_END.items() for g in range(2)}
        GATE_COPY, GATE_PICK, GATE_NORM, GATE_SET = ([gate_at(c) + GU + n for c in range(NCH)] for n in (1, 2, 3, 4))

        block = ctx.enter_context(nc.Block())

        @block.sync
        def _(sp):
            def load_round(b, r, wait):
                if wait:
                    sp.wait_ge(feat_added, b * BLOCK_ROUNDS + (r + 1 - RING_ROUNDS))
                for j in range(CG):
                    rr, jj = divmod(r * CG + j - IN_FLIGHT, CG)
                    if (wait and j) or (rr >= 0 and not wait):
                        sp.wait_ge(x_loaded[rr % RING_ROUNDS][jj], b * 32 + 16 * (rr // RING_ROUNDS + 1))
                    sp.dma_start(xring[:, r % RING_ROUNDS, j, :, :],
                                 x_v[b, r, :, j, :, :]).then_inc(x_loaded[r % RING_ROUNDS][j], 16)

            for r in range(RING_ROUNDS):
                load_round(0, r, False)
            sp.wait_ge(zeroed, 1)
            for a, at, src in ((0, 0, eb1), (0, N1, bn1_g), (0, 2 * N1, eb2), (1, 0, bn1_b), (1, N1, bn2_g),
                               (1, N1 + N2, bn2_b), (1, N1 + 2 * N2, gb1)):
                src = src.rearrange("e (m p) -> (e m) p", p=P)
                sp.dma_start(prm_rows[at:at + src.shape[0], a, :], src).then_inc(prm_loaded, 16)
            sp.dma_start(D_i.bitcast(I32), D.rearrange("(b p) -> b p", p=P)).then_inc(prm_loaded, 16)
            sp.dma_start(gW2_rows, gW2.rearrange("h (m p) e -> (h m) (p e)", p=P)).then_inc(prm_loaded, 16)
            sp.dma_start(hW_rows, hW.rearrange("h (m p) c -> (h m) (p c)", p=P)).then_inc(prm_loaded, 16)
            sp.dma_start(gb2_bc[:, :, :], gb2.partition_broadcast(P)).then_inc(prm_loaded, 16)
            sp.dma_start(hb_bc[:, :, :], hb.partition_broadcast(P)).then_inc(prm_loaded, 16)
            for r in range(RING_ROUNDS, BLOCK_ROUNDS):
                load_round(0, r, True)
            with sp.Fori(1, NBLK) as b:
                for r in range(BLOCK_ROUNDS):
                    load_round(b, r, True)
            sp.wait_ge(out_ready, NCH)
            sp.dma_start(out.rearrange("(b p) c -> p b c", p=P), out_sb[:, :, :]).then_inc(stored, 16)
            sp.wait_ge(stored, 16)

        @block.gpsimd
        def _(pool):
            nc.gpsimd.memset(ident[:, :], 0.0).then_inc(ident_zero, 1)
            pool.wait_ge(ident_zero, 1)
            nc.gpsimd.affine_select(out=ident[:, :], in_=ident[:, :], compare_op=ALU.not_equal, fill=1.0,
                                    base=0, pattern=[[-1, P]], channel_multiplier=1).then_inc(ident_ready, 1)

            def load_unit(it, u0, src):
                if is_split(u0):
                    if u0 >= RAW:
                        pool.wait_ge(lo_ready, splits(it, u0) - RAW)
                    pool.dma_start(wraw[:, raw_slot(u0), :, :], src).then_inc(w_loaded[raw_slot(u0)], 16)
                else:
                    wait_unit_used(pool, it, u0 - EU)
                    pool.dma_start(w2raw[:, u0 % 2, :, :], src).then_inc(w2_loaded[u0 % 2], 16)

            def gate_unit(u0, n):
                head, half = divmod(n, 2)
                load_unit(0, u0, gW1_v[head, :, KU * half:KU * half + KU, :])

            def expert_unit(it, u0, expert, k):
                panel, half = divmod(k, 2)
                ks = slice(KU * half, KU * half + KU)
                if panel < 2:
                    src = eW1_v[expert, :, ks, UNIT_COLS * panel:UNIT_COLS * (panel + 1)]
                else:
                    src = eW2_v[expert, :, ks, :]
                load_unit(it, u0, src)

            for r, units in ((0, range(AHEAD)), (CB * BLOCK_ROUNDS, range(AHEAD, RAW))):
                pool.wait_ge(x_loaded[r % RING_ROUNDS][CG - 1], 16 * (r // RING_ROUNDS + 1))
                for n in units:
                    gate_unit(n, n)
            for s in range(RAW, SLOTS):
                _, n, q, k = ORDER[s]
                if n is not None:
                    gate_unit(s, n)
                else:
                    expert_unit(0, s, q, k)
            with pool.Fori(0, ITERS) as it:
                for n in range(BU):
                    expert_unit(it, SLOTS + n, it * BODY + n // EU, n % EU)
            for n in range(AHEAD):
                expert_unit(0, SLOTS + BU * ITERS + n, 0, n)
            for n in range(AHEAD):
                wait_loaded(pool, 0, SLOTS + BU * ITERS + n)

        @block.scalar
        def _(act):
            act.dma_start(aw_bc[:, :], aw.partition_broadcast(P)).then_inc(aw_loaded, 16)

            def split_hi(it, u0):
                if not is_split(u0):
                    return
                wait_loaded(act, it, u0)
                if u0 >= SPLIT:
                    wait_unit_used(act, it, u0 - SPLIT)
                nc.scalar.activation(whi[:, u0 % SPLIT, :, :], wraw[:, raw_slot(u0), :, :],
                                     ACT.Copy).then_inc(hi_ready, 1)

            def sum_rows(b, r, ts):
                for t in ts:
                    j, i = divmod(t, 2)
                    if i == 0:
                        act.wait_ge(x_loaded[r % RING_ROUNDS][j], b * 32 + 16 * (r // RING_ROUNDS + 1))
                    at = r * ROUND_TILES + t
                    if at >= 2:
                        act.wait_ge(summed, b * (BLOCK_ROUNDS * ROUND_TILES) + (at - 1))
                    if t == 0 and r >= 2:
                        act.wait_ge(mask_ready, b * BLOCK_ROUNDS + (r - 1))
                    nc.scalar.activation(copy_out[:, t % 2, :], xring[:, r % RING_ROUNDS, j, i, :], ACT.Copy,
                                         accum_out=rowsum[:, r % 2, t:t + 1]).then_inc(summed, 1)

            def softmax_exp(b, r):
                act.wait_ge(max_ready, b * BLOCK_ROUNDS + (r + 1))
                for h in range(2):
                    last = nc.scalar.activation(exps[:, h, :], soft_ps[0:ROUND_TILES, L * h:L * h + L], ACT.Exp,
                                                bias=neg_max[:, r % 2, h:h + 1], accum_out=expsum[:, h:h + 1])
                last.then_inc(exp_ready, 1)

            def copy_rows(b):
                act.wait_ge(feat_added, b * BLOCK_ROUNDS + BLOCK_ROUNDS)
                nc.scalar.activation(rows[:, 0:DM // 2], feat_ps[:, 0, 0:DM // 2], ACT.Copy).then_inc(rows_a, 1)

            def features_hi(it, c, j, g, blk):
                act.wait_ge(turned, it * 2 + (FEAT_TURN[c] + 2 * j + g + 1))
                nc.scalar.activation(feat_hi[:, c, KU * g:KU * g + KU, blk],
                                     turned_feat(c, j, g).rearrange("p (k n) -> p k n", k=KU),
                                     ACT.Copy).then_inc(turned_hi, 1)

            def read_h1(it, q, panel0, c, ms):
                panel = expert_at(c, q, 2 * panel0) // 2
                for m in ms:
                    t = MT * panel0 + m
                    act.wait_ge(z_ready, tiles(it, panel, m))
                    col = bass.ds(it * (KT * BODY) + (KT * q + t), 1)
                    nc.scalar.activation(h1[:, t, :], z_ps[:, (MT * panel + m) % ZB, 0:CHUNK], ACT.Relu,
                                         bias=bias[:, col], scale=scale[:, col]).then_inc(z_read, 1)

            def read_h2(it, q, c, ms):
                panel = expert_at(c, q, EU - 2) // 2
                if ms[0] == 0:
                    if c or q:
                        act.wait_ge(rep_added, it * BODY + (E * c + q))
                        if not c and q == E - 1:
                            act.wait_ge(logits_ready, H * NCH)
                    else:
                        act.wait_ge(logits_ready, H)
                for m in ms:
                    act.wait_ge(z_ready, tiles(it, panel, m))
                    col = bass.ds(it * (HT * BODY) + (E * KT + HT * q + m), 1)
                    nc.scalar.activation(h2[:, m, :], z_ps[:, (MT * panel + m) % ZB, 0:CHUNK], ACT.Relu,
                                         bias=bias[:, col], scale=scale[:, col]).then_inc(z_read, 1)

            def read_gate(c, head, ms):
                panel = gate_at(c) // 2 + head
                if ms[0]:
                    pass
                elif head:
                    act.wait_ge(logits_ready, H * c + head)
                elif c:
                    act.wait_ge(rep_added, E - 1)
                else:
                    act.wait_ge(params_ready, 1)
                for m in ms:
                    act.wait_ge(z_ready, tiles(0, panel, m))
                    at = N1 + N2 + HT * head + m
                    nc.scalar.activation(h2[:, m, :], z_ps[:, (MT * panel + m) % ZB, 0:CHUNK], ACT.Relu,
                                         bias=bias[:, at:at + 1]).then_inc(z_read, 1)

            def gate_exp(c):
                act.wait_ge(gmax_ready, c + 1)
                for b in range(CB):
                    last = nc.scalar.activation(gexp[:, b, :], gl[:, b, :], ACT.Exp, bias=gmax[:, b:b + 1],
                                                accum_out=gsum[:, b:b + 1])
                last.then_inc(gexp_ready, 1)

            def head_exp(c):
                act.wait_ge(omax_ready, c + 1)
                for b in range(CB):
                    last = nc.scalar.activation(oexp[:, b, :], ol[:, b, :], ACT.Exp, bias=omax[:, b:b + 1],
                                                accum_out=osum[:, b:b + 1])
                last.then_inc(oexp_ready, 1)

            def expert_reads(it, c, q, k, late):
                if k in (1, 3) and not late:
                    read_h1(it, q, k // 2, c, (0, 1))
                if k in (2, 4) and late:
                    read_h1(it, q, k // 2 - 1, c, (2,))
                if k == 5 and not late:
                    read_h2(it, q, c, (0, 1))
                if k == 0 and q and late:
                    read_h2(it, q - 1, c, (2,))

            def read_last_tile(s):
                c, n, q, k = ORDER[s]
                if n is not None and n % 2:
                    read_gate(c, n // 2, (2,))
                elif k in (1, 3):
                    read_h1(0, q, k // 2, c, (2,))
                elif k == 5:
                    read_h2(0, q, c, (2,))

            def x_third(b, w):
                r, third = divmod(w, 3)
                if r < ROUNDS:
                    sum_rows(b, r, to_score(third))
                if third == 1 and 1 <= r <= ROUNDS:
                    softmax_exp(b, r - 1)

            def x_round(b, r):
                sum_rows(b, r, range(EXP_AT))
                softmax_exp(b, r - 1)
                sum_rows(b, r, range(EXP_AT, ROUND_TILES))

            for w in range(LEAD):
                x_third(0, w)
            for n in range(AHEAD):
                split_hi(0, n)
            with act.Fori(0, CB) as it:
                for r in range(1, BLOCK_ROUNDS + 1):
                    x_round(it, r)
                copy_rows(it)
                for g in range(2):
                    features_hi(it, 0, 0, g, bass.ds(it * P, P))
            for s in range(SLOTS):
                c, n, q, k = ORDER[s]
                reads_first = s >= expert_at(0, SPLIT_FROM, 0)
                if not reads_first:
                    split_hi(0, s + AHEAD)
                if s:
                    read_last_tile(s - 1)
                if reads_first:
                    split_hi(0, s + AHEAD)
                if s in BLOCK_END:
                    copy_rows(CB + BLOCK_END[s])
                for (j, g), t in TURN_SLOT.items():
                    if s == t + 1:
                        features_hi(0, 1, j, g, slice(P * j, P * j + P))
                if s in GATE_NORM:
                    gate_exp(GATE_NORM.index(s))
                x_third(CB - 1, SLOT_THIRD + s)
                if n is not None and n % 2:
                    read_gate(c, n // 2, (0, 1))
                elif k is not None:
                    expert_reads(0, c, q, k, False)
            read_last_tile(SLOTS - 1)
            head_exp(0)
            with act.Fori(0, ITERS) as it:
                for n in range(BU):
                    q, k = divmod(n, EU)
                    expert_reads(it, 1, q, k, True)
                    split_hi(it, SLOTS + n + AHEAD)
                    expert_reads(it, 1, q, k, False)
                read_h2(it, BODY - 1, 1, (2,))
            head_exp(1)

        @block.vector
        def _(dve):
            links = [0]

            def link(ins):
                links[0] += 1
                ins.then_inc(link_dve, 1)
                dve.wait_ge(link_dve, links[0])

            nc.vector.memset(h2[:, :, :], 0.0).then_inc(zeroed, 1)
            nc.vector.memset(pwin[:, :, :], 0.0)
            nc.vector.memset(prob[:, :, :], 0.0)
            nc.vector.memset(rep[:, :, :], 0.0).then_inc(rep_zeroed, 1)

            def split_lo(it, u0):
                if not is_split(u0):
                    return
                dve.wait_ge(hi_ready, splits(it, u0))
                nc.vector.tensor_tensor(wlo[:, u0 % SPLIT, :, :], wraw[:, raw_slot(u0), :, :],
                                        whi[:, u0 % SPLIT, :, :].bitcast(F32), ALU.subtract).then_inc(lo_ready, 1)

            def score_tile(b, r, t):
                j, i = divmod(t, 2)
                if i == 0:
                    dve.wait_ge(x_loaded[r % RING_ROUNDS][j], b * 32 + 16 * (r // RING_ROUNDS + 1))
                at = r * ROUND_TILES + t
                if at >= 2:
                    dve.wait_ge(scored, b * (BLOCK_ROUNDS * ROUND_TILES) + (at - 1))
                nc.vector.tensor_tensor_reduce(
                    out=prod_out[:, t % 2, :], in0=xring[:, r % RING_ROUNDS, j, i, :], in1=aw_bc[:, :], scale=1.0,
                    scalar=0.0, op0=ALU.mult, op1=ALU.add, accum_out=score[:, r % 2, t:t + 1]).then_inc(scored, 1)

            def mask_scores(b, r):
                n = b * BLOCK_ROUNDS + (r + 1)
                dve.wait_ge(summed, n * ROUND_TILES)
                nc.vector.tensor_scalar(penalty[:, :], rowsum[:, r % 2, :], 0.0, -3e38, ALU.is_equal,
                                        ALU.mult).then_inc(pen_ready, 1)
                dve.wait_ge(pen_ready, n)
                dve.wait_ge(scored, n * ROUND_TILES)
                nc.vector.scalar_tensor_tensor(out=masked[:, r % 2, :], in0=penalty[:, :], scalar=3.0,
                                               in1=score[:, r % 2, :], op0=ALU.mult,
                                               op1=ALU.add).then_inc(mask_ready, 1)

            def softmax_max(b, r):
                dve.wait_ge(scores_turned, b * BLOCK_ROUNDS + (r + 1))
                nc.vector.tensor_reduce(neg_max[:, r % 2, :],
                                        soft_ps[0:ROUND_TILES, 0:P].rearrange("t (h l) -> t h l", h=2),
                                        AX.X, ALU.max, negate=True).then_inc(max_ready, 1)

            def softmax_norm(b, r):
                n = b * BLOCK_ROUNDS + (r + 1)
                dve.wait_ge(exp_ready, n)
                nc.vector.reciprocal(recip[:, :], expsum[:, :]).then_inc(recip_ready, 1)
                dve.wait_ge(recip_ready, n)
                nc.vector.tensor_tensor(prob[0:ROUND_TILES, :, :], exps[:, :, :],
                                        recip[:, :].unsqueeze(2).to_broadcast([ROUND_TILES, 2, L]),
                                        ALU.mult).then_inc(prob_ready, 1)

            def place_probs(b, r):
                n = b * BLOCK_ROUNDS + r
                dve.wait_ge(prob_turned, n + 1)
                if r:
                    dve.wait_ge(feat_added, n)
                for h in range(2):
                    p = slice(L * h, L * h + L)
                    last = nc.vector.tensor_copy(pwin[p, :, WIN + h],
                                                 soft_ps[p, P:P + ROUND_TILES])
                last.then_inc(pwin_ready, 1)

            def copy_rows(b):
                dve.wait_ge(feat_added, b * BLOCK_ROUNDS + BLOCK_ROUNDS)
                nc.vector.tensor_copy(rows[:, DM // 2:DM], feat_ps[:, 1, 0:DM // 2]).then_inc(rows_b, 1)

            def features_lo(it, c, j, g, blk):
                dve.wait_ge(turned_hi, it * 2 + (2 * CB * c + 2 * j + g + 1))
                ks = slice(KU * g, KU * g + KU)
                nc.vector.tensor_tensor(feat_lo[:, c, ks, blk],
                                        turned_feat(c, j, g).rearrange("p (k n) -> p k n", k=KU),
                                        feat_hi[:, c, ks, blk].bitcast(F32),
                                        ALU.subtract).then_inc(turned_read, 1)

            def split_h1(it, q, panel0, c, m):
                panel = expert_at(c, q, 2 * panel0) // 2
                t = MT * panel0 + m
                dve.wait_ge(z_read, tiles(it, panel, m))
                nc.vector.tensor_copy(h1_hi[:, t, :], h1[:, t, :]).then_inc(h1_hi_ready, 1)
                dve.wait_ge(h1_hi_ready, h1_splits(it, c, q, t))
                nc.vector.tensor_tensor(h1_lo[:, t, :], h1[:, t, :], h1_hi[:, t, :].bitcast(F32),
                                        ALU.subtract).then_inc(h1_ready, 1)

            def pick_gate(it, q, c):
                n = E * c + q
                if n:
                    dve.wait_ge(gate_bc_ready, it * BODY + n)
                nc.vector.tensor_copy(pick[:, :], ident[0:E, bass.ds(it * BODY + q, 1)].to_broadcast([E, P])
                                      ).then_inc(pick_ready, 1)

            def add_expert(it, q, c):
                n = E * c + q
                panel = expert_at(c, q, EU - 2) // 2
                dve.wait_ge(gate_bc_ready, it * BODY + (n + 1))
                if n:
                    dve.wait_ge(rep_added, it * BODY + n)
                dve.wait_ge(z_read, tiles(it, panel, MT - 1))
                nc.vector.tensor_tensor(h2[:, :, :], h2[:, :, :],
                                        gate_bc.unsqueeze(1).to_broadcast([P, HT, CHUNK]),
                                        ALU.mult).then_inc(gated_ready, 1)
                dve.wait_ge(gated_ready, it * BODY + (n + 1))
                nc.vector.tensor_tensor(rep[:, :, :], rep[:, :, :], h2[:, :, :], ALU.add).then_inc(rep_added, 1)

            def x_third(b, w, s=None):
                r, third = divmod(w, 3)
                scores = to_score(third) if r < ROUNDS else ()
                for t in scores[:1]:
                    score_tile(b, r, t)
                if third == 0 and FIRST_SPREAD <= r - 2 < ROUNDS:
                    place_probs(b, r - 2)
                if third == 0 and 1 <= r <= ROUNDS:
                    mask_scores(b, r - 1)
                if third == 1 and 1 <= r <= ROUNDS:
                    softmax_max(b, r - 1)
                if third == 2 and 1 <= r <= ROUNDS:
                    softmax_norm(b, r - 1)
                if s is not None:
                    split_lo(0, s + AHEAD)
                for t in scores[1:]:
                    score_tile(b, r, t)

            def x_round(b, r):
                for t in range(ROUND_TILES):
                    score_tile(b, r, t)
                    if t == MASK_AT:
                        mask_scores(b, r - 1)
                    if t == MAX_AT:
                        softmax_max(b, r - 1)
                    if t == NORM_AT:
                        softmax_norm(b, r - 1)
                    if t == PLACE_AT:
                        place_probs(b, r - 1)

            def head_pick(c):
                dve.wait_ge(out_logits, c + 1)
                for b in range(CB):
                    link(nc.vector.tensor_tensor(osel[:, b, :, :],
                                                 logit_ps[:, 8 * b:8 * b + 2 * H].rearrange("p (h c) -> p h c", c=2),
                                                 hb_bc[:, :, :], ALU.add))
                    link(nc.vector.tensor_tensor(osel[:, b, :, :], osel[:, b, :, :],
                                                 head_is[:, CB * c + b, :].unsqueeze(2).to_broadcast([P, H, 2]),
                                                 ALU.mult))
                    link(nc.vector.tensor_reduce(ol[:, b, :], osel[:, b, :, :].rearrange("p h c -> p c h"),
                                                 AX.X, ALU.add))
                nc.vector.tensor_reduce(omax[:, :], ol[:, :, :], AX.X, ALU.max, negate=True).then_inc(omax_ready, 1)

            def head_norm(c):
                dve.wait_ge(oexp_ready, c + 1)
                link(nc.vector.reciprocal(orec[:, :], osum[:, :]))
                nc.vector.tensor_tensor(out_sb[:, CB * c:CB * c + CB, :], oexp[:, :, :],
                                        orec[:, :].unsqueeze(2).to_broadcast([P, CB, 2]),
                                        ALU.mult).then_inc(out_ready, 1)

            def gate_copy(c):
                dve.wait_ge(logits_ready, H * (c + 1))
                for h in range(H):
                    rows_h = slice(32 * h, 32 * h + E)
                    last = nc.vector.tensor_copy(glogit[rows_h, :], logit_ps[rows_h, :])
                last.then_inc(gl_ready, 1)

            def gate_pick(c):
                dve.wait_ge(turned, GATE_TURN[c] + 1)
                for b in range(CB):
                    turned_b = turn_ps[:, P * b:P * b + P].rearrange("p (h e) -> p h e", h=H)
                    link(nc.vector.tensor_tensor(gsel[:, b, :, :], turned_b[:, :, 0:E], gb2_bc[:, :, :], ALU.add))
                    link(nc.vector.tensor_tensor(gsel[:, b, :, :], gsel[:, b, :, :],
                                                 head_is[:, CB * c + b, :].unsqueeze(2).to_broadcast([P, H, E]),
                                                 ALU.mult))
                    link(nc.vector.tensor_reduce(gl[:, b, :], gsel[:, b, :, :].rearrange("p h e -> p e h"),
                                                 AX.X, ALU.add))
                nc.vector.tensor_reduce(gmax[:, :], gl[:, :, :], AX.X, ALU.max, negate=True).then_inc(gmax_ready, 1)

            def gate_norm(c):
                dve.wait_ge(gexp_ready, c + 1)
                link(nc.vector.reciprocal(grec[:, :], gsum[:, :]))
                nc.vector.tensor_tensor(gate[:, :, :], gexp[:, :, :],
                                        grec[:, :].unsqueeze(2).to_broadcast([P, CB, E]),
                                        ALU.mult).then_inc(gate_ready, 1)

            def gate_set(c):
                dve.wait_ge(turned, GATE_TURN[c] + 2)
                nc.vector.tensor_copy(gateT[:, :], turned_gate(c)).then_inc(gateT_ready, 1)
                dve.wait_ge(gateT_ready, c + 1)
                dve.wait_ge(rep_zeroed, c + 1)

            def set_params():
                dve.wait_ge(turned, PRM_TURN + 1)
                nc.vector.tensor_copy(gW2_sb[:, :, :],
                                      turn_ps[:, GW2_AT:HW_AT].rearrange("p (e r) -> p r e", e=E))
                nc.vector.tensor_copy(hW_sb[:, :, :], turn_ps[:, HW_AT:D_AT].rearrange("p (c r) -> p r c", c=2))
                for h in range(H):
                    nc.vector.tensor_scalar(head_is[:, :, h], turn_ps[:, D_AT:D_AT + NBLK], float(h), None,
                                            ALU.is_equal)
                nc.vector.tensor_copy(prm[:, 0, 0:2 * N1 + N2], turn_ps[:, 0:2 * N1 + N2])
                nc.vector.tensor_copy(prm[:, 1, 0:N1 + 2 * N2 + H * HT],
                                      turn_ps[:, P:P + N1 + 2 * N2 + H * HT]).then_inc(turned_read, 1)
                dve.wait_ge(turned_read, PRM_TURN + 1)
                nc.vector.tensor_scalar(scale[:, 0:N1], prm[:, 0, N1:2 * N1], BN_SCALE, None, ALU.mult)
                link(nc.vector.tensor_scalar(scale[:, N1:N1 + N2], prm[:, 1, N1:N1 + N2], BN_SCALE, None, ALU.mult))
                nc.vector.tensor_tensor(bias[:, 0:N1], prm[:, 0, 0:N1], scale[:, 0:N1], ALU.mult)
                link(nc.vector.tensor_tensor(bias[:, N1:N1 + N2], prm[:, 0, 2 * N1:2 * N1 + N2], scale[:, N1:N1 + N2],
                                             ALU.mult))
                nc.vector.tensor_tensor(bias[:, 0:N1], bias[:, 0:N1], prm[:, 1, 0:N1], ALU.add)
                nc.vector.tensor_tensor(bias[:, N1:N1 + N2], bias[:, N1:N1 + N2],
                                        prm[:, 1, N1 + N2:N1 + 2 * N2], ALU.add)
                nc.vector.tensor_copy(bias[:, N1 + N2:N1 + N2 + H * HT],
                                      prm[:, 1, N1 + 2 * N2:N1 + 2 * N2 + H * HT]).then_inc(params_ready, 1)

            dve.wait_ge(aw_loaded, 16)
            for w in range(LEAD):
                x_third(0, w)
            for n in range(AHEAD):
                split_lo(0, n)
            with dve.Fori(0, CB) as it:
                for r in range(1, BLOCK_ROUNDS + 1):
                    x_round(it, r)
                copy_rows(it)
                for g in range(2):
                    features_lo(it, 0, 0, g, bass.ds(it * P, P))
            dve.wait_ge(prm_loaded, 16 * 12)
            nc.vector.tensor_copy(D_f, D_i.bitcast(I32)).then_inc(D_ready, 1)
            for s in range(SLOTS):
                c, n, q, k = ORDER[s]
                if q is not None and q >= SPLIT_FROM and k in (2, 4):
                    for m in range(MT):
                        split_h1(0, q, k // 2 - 1, 0, m)
                if s in GATE_COPY:
                    gate_copy(GATE_COPY.index(s))
                if s in GATE_PICK:
                    gate_pick(GATE_PICK.index(s))
                x_third(CB - 1, SLOT_THIRD + s, s)
                if s == 0:
                    set_params()
                if s in BLOCK_END:
                    copy_rows(CB + BLOCK_END[s])
                for (j, g), t in TURN_SLOT.items():
                    if s == t + 1:
                        features_lo(0, 1, j, g, slice(P * j, P * j + P))
                if k == 0 and q:
                    add_expert(0, q - 1, c)
                if s in GATE_NORM:
                    gate_norm(GATE_NORM.index(s))
                if s in GATE_SET:
                    gate_set(GATE_SET.index(s))
                if k == 4:
                    pick_gate(0, q, c)
            add_expert(0, E - 1, 0)
            head_pick(0)
            head_norm(0)
            nc.vector.memset(rep[:, :, :], 0.0).then_inc(rep_zeroed, 1)
            gate_set(1)
            with dve.Fori(0, ITERS) as it:
                for n in range(BU):
                    q, k = divmod(n, EU)
                    if k in (2, 4):
                        for m in range(MT):
                            split_h1(it, q, k // 2 - 1, 1, m)
                    split_lo(it, SLOTS + n + AHEAD)
                    if k == 4:
                        pick_gate(it, q, 1)
                    if k == 0 and q:
                        add_expert(it, q - 1, 1)
                add_expert(it, BODY - 1, 1)
            head_pick(1)
            head_norm(1)

        @block.tensor
        def _(pe):
            def products(psum_tile, w_hi, w_lo, a_hi, a_lo, first, last):
                nc.tensor.matmul(psum_tile, w_hi, a_hi, start=first, stop=False)
                nc.tensor.matmul(psum_tile, w_hi, a_lo, start=False, stop=False)
                return nc.tensor.matmul(psum_tile, w_lo, a_hi, start=False, stop=last)

            def unit(it, u0, a_hi, a_lo, h1_at=None):
                panel, half = divmod(u0, 2)
                slot = u0 % SPLIT
                if is_split(u0):
                    pe.wait_ge(lo_ready, splits(it, u0))
                else:
                    wait_loaded(pe, it, u0)
                for m in range(MT):
                    z = z_ps[:, (MT * panel + m) % ZB, 0:CHUNK]
                    cols = slice(P * m, P * m + P)
                    if half == 0 and MT * panel + m >= ZB:
                        pe.wait_ge(z_read, tiles(it, panel, m) - ZB)
                    for k in range(KU):
                        kk = KU * half + k
                        if is_split(u0):
                            if h1_at is not None and m == 0:
                                pe.wait_ge(h1_ready, h1_splits(it, *h1_at, kk))
                            last = products(z, whi[:, slot, k, cols], wlo[:, slot, k, cols], a_hi[:, kk, :],
                                            a_lo[:, kk, :], kk == 0, kk == KT - 1)
                        else:
                            if m == 0:
                                pe.wait_ge(z_read, tiles(it, panel - 2 + kk // MT, kk % MT))
                            last = nc.tensor.matmul(z, w2raw[:, half, k, cols], h1[:, kk, :], start=(kk == 0),
                                                    stop=(kk == KT - 1))
                    if half == 1:
                        last.then_inc(z_ready, 1)
                if half == 0:
                    last.then_inc(half_used, 1)

            def turn_scores(b, r):
                n = b * BLOCK_ROUNDS + (r + 1)
                pe.wait_ge(mask_ready, n)
                nc.tensor.transpose(soft_ps[0:ROUND_TILES, 0:P], masked[:, r % 2, :],
                                    ident[:, :]).then_inc(scores_turned, 1)

            def turn_probs(b, r):
                n = b * BLOCK_ROUNDS + (r + 1)
                pe.wait_ge(prob_ready, n)
                nc.tensor.transpose(soft_ps[:, P:2 * P], prob[:, :, :].rearrange("t h l -> t (h l)"),
                                    ident[:, :]).then_inc(prob_turned, 1)

            def add_features(b, r, between=None):
                pe.wait_ge(pwin_ready, b * BLOCK_ROUNDS + (r + 1))
                in_block = r % BLOCK_ROUNDS
                if r and in_block == 0:
                    pe.wait_ge(rows_a, b + r // BLOCK_ROUNDS)
                    pe.wait_ge(rows_b, b + r // BLOCK_ROUNDS)
                for i in range(2):
                    if i and between is not None:
                        turn_scores(b, between)
                    at = WIN - (4 * in_block + 2 * i)
                    for half in range(2):
                        for j in range(CG):
                            last = nc.tensor.matmul(feat_ps[32 * j:32 * j + 32, half, 0:DM // 2],
                                                    pwin[:, 2 * j + i, at:at + 32],
                                                    xring[:, r % RING_ROUNDS, j, i, DM // 2 * half:DM // 2 * (half + 1)],
                                                    start=(in_block == 0 and i == 0),
                                                    stop=(in_block == BLOCK_ROUNDS - 1 and i == 1),
                                                    tile_position=(0, 32 * j))
                last.then_inc(feat_added, 1)

            def turn_features(b, it, c, j, g):
                if g == 0:
                    pe.wait_ge(rows_a, b + 1)
                    pe.wait_ge(rows_b, b + 1)
                    if c:
                        pe.wait_ge(gated_ready, BLOCK_GATED[j])
                elif c and j < CB - 1:
                    pe.wait_ge(turned_read, it * 2 + (FEAT_READ[c] + 2 * j + 1))
                for k in range(KU):
                    last = nc.tensor.transpose(turned_feat(c, j, g)[:, P * k:P * k + P],
                                               rows[:, KU * g + k:DM:KT], ident[:, :])
                last.then_inc(turned, 1)

            def gate_broadcast(it, q, c):
                n = E * c + q
                pe.wait_ge(pick_ready, it * BODY + (n + 1))
                if n:
                    pe.wait_ge(gated_ready, it * BODY + n)
                if c == 0:
                    done = sum(2 for t in BLOCK_END if GU + EU * q + 5 >= t)
                    if done:
                        pe.wait_ge(turned_read, FEAT_READ[1] + done)
                pe.wait_ge(params_ready, 1)
                nc.tensor.matmul(gate_bc, pick[:, :], gateT[:, :], start=True, stop=True).then_inc(gate_bc_ready, 1)

            def x_third(b, w):
                r, third = divmod(w, 3)
                if third == 0 and 1 <= r <= ROUNDS:
                    turn_scores(b, r - 1)
                if third == 1 and FIRST_SPREAD <= r - 2 < ROUNDS:
                    add_features(b, r - 2)
                if third == 2 and 1 <= r <= ROUNDS:
                    turn_probs(b, r - 1)

            def expert_unit(it, c, q, k):
                u0 = expert_at(c, q, k)
                if k < 4:
                    unit(it, u0, feat_hi[:, c, :, :], feat_lo[:, c, :, :])
                else:
                    unit(it, u0, h1_hi, h1_lo, (c, q))
                if k == 5:
                    gate_broadcast(it, q, c)

            def gate_logits(c, head):
                panel = gate_at(c) // 2 + head
                pe.wait_ge(z_read, tiles(0, panel, MT - 1))
                if head == 0 and not c:
                    pe.wait_ge(params_ready, 1)
                if head == 0 and c:
                    pe.wait_ge(gated_ready, E - 1)
                for m in range(HT):
                    last = nc.tensor.matmul(logit_ps[32 * head:32 * head + E, :], gW2_sb[:, HT * head + m, :],
                                            h2[:, m, :], start=(m == 0), stop=(m == HT - 1),
                                            tile_position=(0, 32 * head))
                last.then_inc(logits_ready, 1)

            def head_logits(c):
                pe.wait_ge(rep_added, E * (c + 1))
                pe.wait_ge(gl_ready, NCH)
                for b in range(CB):
                    for m in range(HT):
                        last = nc.tensor.matmul(logit_ps[:, 8 * b:8 * b + 2 * H], rep[:, m, P * b:P * b + P],
                                                hW_m[:, m, :, :], start=(m == 0),
                                                stop=(m == HT - 1))
                last.then_inc(out_logits, 1)

            def turn_gate_logits(c):
                pe.wait_ge(gl_ready, c + 1)
                for b in range(CB):
                    last = nc.tensor.transpose(turn_ps[:, P * b:P * b + P], glogit[:, P * b:P * b + P], ident[:, :])
                last.then_inc(turned, 1)

            def turn_gate(c):
                pe.wait_ge(gate_ready, c + 1)
                for b in range(CB):
                    last = nc.tensor.transpose(turned_gate(c)[:, P * b:P * b + P], gate[:, b, :], ident[:, :])
                last.then_inc(turned, 1)

            def turn_params():
                pe.wait_ge(prm_loaded, 16 * 12)
                pe.wait_ge(D_ready, 1)
                pe.wait_ge(turned_read, PRM_TURN)
                for a, n in ((0, 2 * N1 + N2), (1, N1 + 2 * N2 + H * HT)):
                    nc.tensor.transpose(turn_ps[:, P * a:P * a + n], prm_rows[0:n, a, :], ident[0:n, 0:n])
                n = H * HT
                for src, cols, at in ((gW2_rows, E, GW2_AT), (hW_rows, 2, HW_AT)):
                    for e in range(cols):
                        nc.tensor.transpose(turn_ps[:, at + n * e:at + n * e + n], src[:, e::cols], ident[0:n, 0:n])
                last = nc.tensor.transpose(turn_ps[:, D_AT:D_AT + NBLK], D_f, ident[0:NBLK, 0:NBLK])
                last.then_inc(turned, 1)

            pe.wait_ge(ident_ready, 1)
            with pe.Fori(0, CB) as it:
                turn_scores(it, 0)
                for r in range(BLOCK_ROUNDS):
                    turn_probs(it, r)
                    add_features(it, r, r + 1 if r < BLOCK_ROUNDS - 1 else None)
                for g in range(2):
                    turn_features(it, it, 0, 0, g)
            for s in range(SLOTS):
                c, n, q, k = ORDER[s]
                if n == 0:
                    pe.wait_ge(turned_read, FEAT_READ[c] + 2 * CB)
                if n is not None:
                    unit(0, s, feat_hi[:, c, :, :], feat_lo[:, c, :, :])
                    if s == 0:
                        turn_params()
                else:
                    expert_unit(0, c, q, k)
                for g in range(NCH):
                    head, odd = divmod(s - gate_at(g) - 2, 2)
                    if not odd and 0 <= head < H:
                        gate_logits(g, head)
                if s in GATE_COPY:
                    turn_gate_logits(GATE_COPY.index(s))
                if s in GATE_NORM:
                    turn_gate(GATE_NORM.index(s))
                x_third(CB - 1, SLOT_THIRD + s)
                for (j, g), t in TURN_SLOT.items():
                    if s == t:
                        turn_features(CB + j, 0, 1, j, g)
            head_logits(0)
            with pe.Fori(0, ITERS) as it:
                for n in range(BU):
                    expert_unit(it, 1, *divmod(n, EU))
            head_logits(1)


_INS = ["r_x", "r_D"] + ["L0_rec_" + n for n in ("aw", "gW1", "gb1", "gW2", "gb2", "eW1", "eb1", "bn1_g", "bn1_b",
                                                 "eW2", "eb2", "bn2_g", "bn2_b", "hW", "hb")]
_OUTS = [((512, 2), "float32")]


def kernel(**inputs):
    import numpy as _np
    import concourse.bacc as _bacc
    from concourse import mybir as _mybir
    from concourse.bass_utils import run_bass_kernel_spmd as _run

    nc = _bacc.Bacc("TRN2", target_bir_lowering=False, num_devices=1)
    arrays, args = {}, []
    for name in _INS:
        a = _np.ascontiguousarray(inputs[name])
        arrays[f"in_{name}_dram"] = a
        args.append(nc.dram_tensor(f"in_{name}_dram", a.shape, _mybir.dt.from_np(a.dtype), kind="ExternalInput").ap())
    for i, (shape, dtype) in enumerate(_OUTS):
        dt = _mybir.dt.from_np(_np.dtype(dtype))
        args.append(nc.dram_tensor(f"out_{i}_dram", shape, dt, kind="ExternalOutput").ap())
    rec_kernel(nc, *args)
    r = _run(nc, [arrays], core_ids=[0])
    return r.results[0]["out_0_dram"]
```
